# Optimizing a Trainium2 kernel written in Bass

```python
import numpy as np
import jax
import jax.numpy as jnp

def _softmax(x, axis=-1):
    return jax.nn.softmax(x, axis=axis)

def _gelu(x):
    return jax.nn.gelu(x, approximate=True)

def _silu(x):
    return jax.nn.silu(x)

def _sigmoid(x):
    return jax.nn.sigmoid(x)

def _layernorm(x, axis=-1, eps=1e-05):
    m = jnp.mean(x, axis=axis, keepdims=True)
    v = jnp.var(x, axis=axis, keepdims=True)
    return (x - m) / jnp.sqrt(v + eps)

def _scatter_add(tgt, idx, src, axis=0):
    return tgt.at[idx].add(src)

def _segment_sum(src, seg, n):
    return jax.ops.segment_sum(src, seg, n)
kernel_name = 'mk_xattn_ffn_d1_seqx_r4_da4cec'

def setup_inputs(seed: int=0):
    np.random.seed(seed)
    _w = jnp.asarray

    def _rec_inputs():
        import jax
        import jax.numpy as jnp
        _rk = jax.random.key(seed)
        x = 7.22e-05 + 1 * jax.random.normal(jax.random.fold_in(_rk, 1), (16, 100, 256), jnp.float32)
        _lenS = 100 - jax.random.randint(jax.random.fold_in(_rk, 7), (16,), 0, max(1, 100 // 4) + 1, jnp.int32)
        _lenS2 = 361 - jax.random.randint(jax.random.fold_in(_rk, 8), (16,), 0, max(1, 361 // 4) + 1, jnp.int32)
        _ctx_1024P = jax.random.normal(jax.random.fold_in(_rk, 11), (16, 16, 256), jnp.float32)
        _ctx_1024c = jax.random.dirichlet(jax.random.fold_in(_rk, 511), 0.3 * jnp.ones((16,), jnp.float32), (16, 361))
        _ctx_1024t = jnp.einsum('bsk,bkd->bsd', _ctx_1024c, _ctx_1024P)
        _ctx_1024t = _ctx_1024t * jax.lax.rsqrt(jnp.mean(jnp.square(_ctx_1024t)) + 1e-12) * 0.953939
        ctx_1024 = 4.13588e-05 + 0.999923 * (_ctx_1024t + 0.3 * jax.random.normal(jax.random.fold_in(_rk, 611), (16, 361, 256), jnp.float32))
        return (x, ctx_1024)
    x, ctx_1024 = _rec_inputs()

    def _L0_xattn_setup():
        import jax, jax.numpy as jnp
        import numpy as np
        D_MODEL = 256
        NUM_HEAD = 16
        HEAD_DIM = D_MODEL // NUM_HEAD
        B, S = (4, 512)
        key = jax.random.key(seed)
        ks = jax.random.split(key, 8)
        sc = 0.02
        return {'q_in': jax.random.normal(ks[0], (B, S, D_MODEL), jnp.float32), 'k_in': jax.random.normal(ks[1], (B, S, D_MODEL), jnp.float32), 'v_in': jax.random.normal(ks[2], (B, S, D_MODEL), jnp.float32), 'Wq': jax.random.normal(ks[3], (D_MODEL, D_MODEL), jnp.float32) * sc, 'bq': jnp.zeros((D_MODEL,), jnp.float32), 'Wk': jax.random.normal(ks[4], (D_MODEL, D_MODEL), jnp.float32) * sc, 'bk': jnp.zeros((D_MODEL,), jnp.float32), 'Wv': jax.random.normal(ks[5], (D_MODEL, D_MODEL), jnp.float32) * sc, 'bv': jnp.zeros((D_MODEL,), jnp.float32), 'Wo': jax.random.normal(ks[6], (D_MODEL, D_MODEL), jnp.float32) * sc, 'bo': jnp.zeros((D_MODEL,), jnp.float32)}
    _L0_xattn_all = _L0_xattn_setup()
    _L0_xattn_in = {k: v for k, v in _L0_xattn_all.items() if k in ('Wq', 'bq', 'Wk', 'bk', 'Wv', 'bv', 'Wo', 'bo')}
    del _L0_xattn_all

    def _L0_ffn_setup():
        import jax, jax.numpy as jnp
        import numpy as np
        E = 32
        H = 256
        I = 128
        G = 8
        TKG = 4
        TOPK = 8
        NSH = 2
        SCALE = 2.5
        key = jax.random.key(seed)
        ks = jax.random.split(key, 10)
        s = 0.02
        return {'hidden_states': jax.random.normal(ks[0], (2, 256, H), jnp.float32), 'gate_w': jax.random.normal(ks[1], (E, H), jnp.float32) * s, 'gate_bias': jax.random.normal(ks[2], (E,), jnp.float32) * s, 'w_gate': jax.random.normal(ks[3], (E, I, H), jnp.float32) * s, 'w_up': jax.random.normal(ks[4], (E, I, H), jnp.float32) * s, 'w_down': jax.random.normal(ks[5], (E, H, I), jnp.float32) * s, 'sh_gate': jax.random.normal(ks[6], (I * NSH, H), jnp.float32) * s, 'sh_up': jax.random.normal(ks[7], (I * NSH, H), jnp.float32) * s, 'sh_down': jax.random.normal(ks[8], (H, I * NSH), jnp.float32) * s}
    _L0_ffn_all = _L0_ffn_setup()
    _L0_ffn_in = {k: v for k, v in _L0_ffn_all.items() if k in ('gate_w', 'gate_bias', 'w_gate', 'w_up', 'w_down', 'sh_gate', 'sh_up', 'sh_down')}
    del _L0_ffn_all
    return {'x': x, 'ctx_1024': ctx_1024, 'L0_xattn_Wq': _L0_xattn_in['Wq'], 'L0_xattn_bq': _L0_xattn_in['bq'], 'L0_xattn_Wk': _L0_xattn_in['Wk'], 'L0_xattn_bk': _L0_xattn_in['bk'], 'L0_xattn_Wv': _L0_xattn_in['Wv'], 'L0_xattn_bv': _L0_xattn_in['bv'], 'L0_xattn_Wo': _L0_xattn_in['Wo'], 'L0_xattn_bo': _L0_xattn_in['bo'], 'L0_ffn_gate_w': _L0_ffn_in['gate_w'], 'L0_ffn_gate_bias': _L0_ffn_in['gate_bias'], 'L0_ffn_w_gate': _L0_ffn_in['w_gate'], 'L0_ffn_w_up': _L0_ffn_in['w_up'], 'L0_ffn_w_down': _L0_ffn_in['w_down'], 'L0_ffn_sh_gate': _L0_ffn_in['sh_gate'], 'L0_ffn_sh_up': _L0_ffn_in['sh_up'], 'L0_ffn_sh_down': _L0_ffn_in['sh_down']}

def reference(x, ctx_1024, L0_xattn_Wq, L0_xattn_bq, L0_xattn_Wk, L0_xattn_bk, L0_xattn_Wv, L0_xattn_bv, L0_xattn_Wo, L0_xattn_bo, L0_ffn_gate_w, L0_ffn_gate_bias, L0_ffn_w_gate, L0_ffn_w_up, L0_ffn_w_down, L0_ffn_sh_gate, L0_ffn_sh_up, L0_ffn_sh_down):
    import jax
    import jax.numpy as jnp

    def _L0_xattn_ref(q_in, k_in, v_in, Wq, bq, Wk, bk, Wv, bv, Wo, bo):
        import jax, jax.numpy as jnp
        import numpy as np
        D_MODEL = 256
        NUM_HEAD = 16
        HEAD_DIM = D_MODEL // NUM_HEAD
        B, S = (4, 512)
        b, sq, _ = q_in.shape
        sk = k_in.shape[1]
        Q = q_in @ Wq + bq
        K = k_in @ Wk + bk
        V = v_in @ Wv + bv
        Q = Q.reshape(b, sq, NUM_HEAD, HEAD_DIM).transpose(0, 2, 1, 3)
        K = K.reshape(b, sk, NUM_HEAD, HEAD_DIM).transpose(0, 2, 1, 3)
        V = V.reshape(b, sk, NUM_HEAD, HEAD_DIM).transpose(0, 2, 1, 3)
        scale = 1.0 / jnp.sqrt(jnp.float32(HEAD_DIM))
        scores = jnp.einsum('bhqd,bhkd->bhqk', Q, K) * scale
        causal = jnp.arange(sk)[None, :] <= jnp.arange(sq)[:, None]
        scores = jnp.where(causal[None, None], scores, -jnp.inf)
        attn = jax.nn.softmax(scores, axis=-1)
        out = jnp.einsum('bhqk,bhkd->bhqd', attn, V)
        out = out.transpose(0, 2, 1, 3).reshape(b, sq, D_MODEL)
        return out @ Wo + bo

    def _L0_ffn_ref(hidden_states, gate_w, gate_bias, w_gate, w_up, w_down, sh_gate, sh_up, sh_down):
        import jax, jax.numpy as jnp
        import numpy as np
        E = 32
        H = 256
        I = 128
        G = 8
        TKG = 4
        TOPK = 8
        NSH = 2
        SCALE = 2.5
        B, S, Hd = hidden_states.shape
        h = hidden_states.reshape(-1, Hd)
        logits = h.astype(jnp.float32) @ gate_w.T
        scores = jax.nn.sigmoid(logits)
        sc = scores + gate_bias
        grp = sc.reshape(-1, G, E // G)
        group_scores = jax.lax.top_k(grp, 2)[0].sum(-1)
        gidx = jax.lax.top_k(group_scores, TKG)[1]
        gmask = jnp.sum(jax.nn.one_hot(gidx, G, dtype=sc.dtype), axis=1)
        smask = jnp.repeat(gmask, E // G, axis=1)
        masked = jnp.where(smask > 0, sc, jnp.zeros_like(sc))
        tki = jax.lax.top_k(masked, TOPK)[1]
        tkw = jnp.take_along_axis(scores, tki, axis=1)
        tkw = tkw / (tkw.sum(-1, keepdims=True) + 1e-20)
        tkw = tkw * SCALE
        combine = (jax.nn.one_hot(tki, E, dtype=tkw.dtype) * tkw[..., None]).sum(1)
        g = jax.nn.silu(jnp.einsum('th,eih->tei', h, w_gate))
        u = jnp.einsum('th,eih->tei', h, w_up)
        routed = jnp.einsum('tei,ehi->th', g * u * combine[:, :, None], w_down)
        sg = jax.nn.silu(h @ sh_gate.T)
        shared = sg * (h @ sh_up.T) @ sh_down.T
        return (routed + shared).reshape(B, S, Hd)
    x = x + _L0_xattn_ref(_layernorm(x, axis=-1), ctx_1024, ctx_1024, L0_xattn_Wq, L0_xattn_bq, L0_xattn_Wk, L0_xattn_bk, L0_xattn_Wv, L0_xattn_bv, L0_xattn_Wo, L0_xattn_bo)
    x = x + _L0_ffn_ref(_layernorm(x, axis=-1), L0_ffn_gate_w, L0_ffn_gate_bias, L0_ffn_w_gate, L0_ffn_w_up, L0_ffn_w_down, L0_ffn_sh_gate, L0_ffn_sh_up, L0_ffn_sh_down)
    return x

_drawn_inputs = setup_inputs


def setup_inputs(seed=0):
    import zlib

    import numpy as np

    out = dict(_drawn_inputs(seed))
    spreads = {'L0_xattn_bq': (0.0, 0.8),
     'L0_xattn_bk': (0.0, 0.8),
     'L0_xattn_bv': (0.0, 0.1),
     'L0_xattn_bo': (0.0, 0.1)}
    factors = {'L0_xattn_Wq': 8.0,
     'L0_xattn_Wk': 8.0,
     'L0_ffn_gate_w': 6.272,
     'L0_ffn_gate_bias': 8.0,
     'L0_ffn_w_gate': 5.441,
     'L0_ffn_w_up': 5.365,
     'L0_ffn_w_down': 5.372,
     'L0_ffn_sh_gate': 3.417,
     'L0_ffn_sh_up': 3.382,
     'L0_ffn_sh_down': 3.375}
    for name, (base, spread) in spreads.items():
        noise = np.random.default_rng([zlib.crc32(name.encode()), seed]).standard_normal(out[name].shape)
        drawn = base * np.exp(spread * noise) if base else spread * noise
        out[name] = jnp.asarray(drawn.astype(out[name].dtype))
    for name, factor in factors.items():
        out[name] = (out[name] * factor).astype(out[name].dtype)
    return out
```

```python
from contextlib import ExitStack

import concourse.bass as bass
from concourse import mybir

ALU = mybir.AluOpType
ACT = mybir.ActivationFunctionType
AX = mybir.AxisListType
F32 = mybir.dt.float32
F32R = mybir.dt.float32r
BF16 = mybir.dt.bfloat16

P = 128
D = 256
KC = D // P
NB = 16
S = 100
NG = 4
BG = NB // NG
TG = BG * S
T = NB * S
NH = 16
DH = D // NH
PAIRS = 4
VW = DH + 2
NE = 32
NX = NE + 2
FI = 128
NGRP = 8
EPG = NE // NGRP
TOPG = 4
EPS = 1e-5
ROUTE_SCALE = 2.5
HALVES = 2
CPH = 2
STEPS = NX * CPH
CST = P + TG + 2 + NGRP * NGRP + BG
MASKED = -1e30
TAKEN = -3e38
VECTOR_STEPS = 59


def block_kernel(nc, x, ctx_t, w_attn, w_gate_t, col_bias, row_bias, gate_bias, w_exp, consts, out_t):
    comb = nc.dram_tensor("combine_rows", (NX, T), F32).ap()

    with ExitStack() as top:
        sem = lambda name: top.enter_context(nc.semaphore(name))

        keep = lambda name, shape, dt=F32: top.enter_context(nc.sbuf_tensor(name, shape, dt))
        x1t_all = keep("x1t_all", [P, KC, T])
        h_hi_all = keep("h_hi_all", [P, KC, T], F32R)
        h_lo_all = keep("h_lo_all", [P, KC, T], F32R)
        w_raw = keep("w_raw", [P, 2, 3 * D])
        ps = top.enter_context(nc.psum_tensor("ps", [P, 8, 512], F32))

        part = ExitStack()
        tmp = lambda name, shape, dt=F32: part.enter_context(nc.sbuf_tensor(name, shape, dt))
        cst = tmp("cst", [P, CST])
        ident = cst[:, 0:128]
        mask_f = cst[:, 128:128 + TG]
        pair_mask = cst[:, 528:530]
        earlier = cst[0:S, 530:594]
        minus_half = cst[0:S, 594:598]
        ident_r = tmp("ident_r", [S, S], F32R)
        ident_b = tmp("ident_b", [S, S], BF16)
        mask_b = tmp("mask_b", [S, TG], BF16)
        wa = tmp("wa", [P, 4, KC, D])
        wa_hi = tmp("wa_hi", [P, 4, KC, D], F32R)
        wa_lo = tmp("wa_lo", [P, 4, KC, D], F32R)
        wg = tmp("wg", [P, KC, NE])
        wg_hi = tmp("wg_hi", [P, KC, NE], F32R)
        wg_lo = tmp("wg_lo", [P, KC, NE], F32R)
        cb_qk = tmp("cb_qk", [P, 2, KC])
        rb_vo = tmp("rb_vo", [S, 2, D])
        gb = tmp("gb", [S, NE])
        half_rows = tmp("half_rows", [2, T])
        x_g = tmp("x_g", [S, BG, D])
        xb = tmp("xb", [S, BG, D])
        ctx_f = tmp("ctx_f", [P, KC, TG])
        ctx_hi = tmp("ctx_hi", [P, KC, TG], F32R)
        ctx_lo = tmp("ctx_lo", [P, KC, TG], F32R)
        st = tmp("st", [S, BG, 6])
        mv = tmp("mv", [S, BG, 2])
        ve = tmp("ve", [S, BG])
        rstd = tmp("rstd", [S, BG])
        xn = tmp("xn", [S, BG, D])
        xt_hi = tmp("xt_hi", [P, KC, TG], F32R)
        xt_lo = tmp("xt_lo", [P, KC, TG], F32R)
        k_hi = tmp("k_hi", [P, KC, TG], F32R)
        k_lo = tmp("k_lo", [P, KC, TG], F32R)
        qf = tmp("qf", [P, KC, TG])
        q_hi = [tmp(f"q_hi{i}", [P, KC, TG], F32R) for i in range(2)]
        q_lo = [tmp(f"q_lo{i}", [P, KC, TG], F32R) for i in range(2)]
        vf = tmp("vf", [S, BG, D])
        v_hi = tmp("v_hi", [S, BG, NH, VW], F32R)
        v_lo = tmp("v_lo", [S, BG, NH, VW], F32R)
        pad_f = tmp("pad_f", [S, BG, NH, 2])
        nm = tmp("nm", [S, NH])
        nm_hi = tmp("nm_hi", [S, NH], F32R)
        nm_lo = tmp("nm_lo", [S, NH], F32R)
        prob = tmp("prob", [S, 2, NH * S])
        pt_hi = tmp("pt_hi", [S, 2, 4 * S], F32R)
        pt_lo = tmp("pt_lo", [S, 2, 4 * S], F32R)
        rden = tmp("rden", [S, NH])
        on = tmp("on", [S, D])
        ot_hi = tmp("ot_hi", [P, KC, S], F32R)
        ot_lo = tmp("ot_lo", [P, KC, S], F32R)
        x1 = tmp("x1", [S, BG, D])
        h1 = tmp("h1", [S, BG, D])
        h_hi = tmp("h_hi", [P, KC, TG], F32R)
        h_lo = tmp("h_lo", [P, KC, TG], F32R)
        rt = tmp("rt", [S, 12, BG * NE])
        pair_max = tmp("pair_max", [S, BG * NGRP, 2])
        pair_min = tmp("pair_min", [S, BG * NGRP, 2])
        gs = tmp("gs", [S, 4, BG * NGRP])
        cmpa = tmp("cmpa", [S, BG, NGRP, NGRP])
        cmpb = tmp("cmpb", [S, BG, NGRP, NGRP])
        best = tmp("best", [S, BG, 8])
        wsum = tmp("wsum", [S, 2, BG])
        comb_t = tmp("comb_t", [NE, TG])
        part.close()

        w_hi = keep("w_hi", [P, 2, 3 * D], F32R)
        w_lo = keep("w_lo", [P, 2, 3 * D], F32R)
        cw = keep("cw", [P, 2, CPH * TG])
        act = keep("act", [P, 4, TG])
        a_hi = keep("a_hi", [P, 4, TG], F32R)
        a_lo = keep("a_lo", [P, 4, TG], F32R)
        y_out = keep("y_out", [P, 4, TG])
        zero_b = keep("zero_b", [P, TG], BF16)

        const_in = sem("const_in"); weight_in = sem("weight_in"); bias_in = sem("bias_in")
        x_in = sem("x_in"); ctx_in = sem("ctx_in")
        const_cast = sem("const_cast"); w_hi_ready = sem("w_hi_ready"); w_lo_ready = sem("w_lo_ready")
        v_pad = sem("v_pad"); half_ready = sem("half_ready"); half_out = sem("half_out")
        var_ready = sem("var_ready"); rstd_ready = sem("rstd_ready"); xn_ready = sem("xn_ready")
        xt_psum = sem("xt_psum"); xt_hi_ready = sem("xt_hi_ready"); xt_lo_ready = sem("xt_lo_ready")
        ctx_hi_ready = sem("ctx_hi_ready"); ctx_lo_ready = sem("ctx_lo_ready")
        k_psum = sem("k_psum"); k_hi_ready = sem("k_hi_ready"); k_lo_ready = sem("k_lo_ready")
        v_psum = sem("v_psum"); vf_ready = sem("vf_ready"); v_hi_ready = sem("v_hi_ready"); v_lo_ready = sem("v_lo_ready")
        q_psum = sem("q_psum"); qf_ready = sem("qf_ready"); q_ready = sem("q_ready"); xb_ready = sem("xb_ready")
        score_psum = sem("score_psum"); nm_ready = sem("nm_ready"); shifted = sem("shifted"); prob_ready = sem("prob_ready")
        pt_psum = sem("pt_psum"); pt_hi_ready = sem("pt_hi_ready"); pt_lo_ready = sem("pt_lo_ready")
        pv_quarter = sem("pv_quarter"); on_ready = sem("on_ready")
        ot_psum = sem("ot_psum"); ot_hi_ready = sem("ot_hi_ready"); ot_lo_ready = sem("ot_lo_ready")
        proj_psum = sem("proj_psum"); x1_ready = sem("x1_ready")
        var2_ready = sem("var2_ready"); rstd2_ready = sem("rstd2_ready"); h1_ready = sem("h1_ready")
        ht_psum = sem("ht_psum"); x1t_psum = sem("x1t_psum"); h_hi_ready = sem("h_hi_ready"); h_lo_ready = sem("h_lo_ready")
        x1t_ready = sem("x1t_ready"); h_kept = sem("h_kept")
        logit_psum = sem("logit_psum"); tanh_ready = sem("tanh_ready"); cmb_ready = sem("cmb_ready")
        cmbt_psum = sem("cmbt_psum"); cmbt_ready = sem("cmbt_ready"); cmb_out = sem("cmb_out")
        step = sem("vector_step")
        wr_in = [sem(f"wr_in{i}") for i in range(2)]; cw_in = [sem(f"cw_in{i}") for i in range(2)]
        gu_hi = sem("gu_hi"); gu_lo = sem("gu_lo"); dn_hi = sem("dn_hi"); dn_lo = sem("dn_lo")
        gu_psum = sem("gu_psum"); tanh_e = sem("tanh_e"); opened = sem("opened"); gated = sem("gated"); weighted = sem("weighted")
        a_hi_ready = sem("a_hi_ready"); a_lo_ready = sem("a_lo_ready"); down_done = sem("down_done")
        zero_ready = sem("zero_ready"); y_ready = sem("y_ready"); y_stored = sem("y_stored")

        block = top.enter_context(nc.Block())
        f = lambda ap: ap.bitcast(F32)

        def wait_alone(eng, semaphore, value, met, met_value):
            value = value if isinstance(value, int) else eng.snap(eng.to_reg(value))
            eng.wait_ge(met, met_value)
            eng.wait_ge(semaphore, value)

        def attention_over(eng):
            eng.wait_ge(cmbt_ready, NG)
            eng.wait_ge(h_kept, 32 * NG + 1)
            eng.wait_ge(cmb_out, 16 * NG + 1)

        @block.sync
        def _(sp):
            sp.sem_inc(h_kept, 1)
            sp.sem_inc(cmb_out, 1)
            sp.dma_start(cst[:], consts).then_inc(const_in, 16)
            sp.dma_start(wa[:], w_attn).then_inc(weight_in, 16)
            sp.dma_start(wg[:], w_gate_t).then_inc(weight_in, 16)
            sp.dma_start(cb_qk[:], col_bias).then_inc(bias_in, 16)
            sp.dma_start(rb_vo[:], row_bias.rearrange("(o a) d -> o a d", o=1).to_broadcast([S, 2, D])).then_inc(bias_in, 16)
            sp.dma_start(gb[:], gate_bias.rearrange("(o e) -> o e", o=1).to_broadcast([S, NE])).then_inc(bias_in, 16)
            sp.wait_ge(half_ready, 1)
            sp.dma_start(comb[NE:NX, :], half_rows[:]).then_inc(half_out, 16)

            def loads(g):
                sp.dma_start(x_g[:], x[:, bass.ds(g * BG, BG), :]).then_inc(x_in, 16)
                sp.dma_start(ctx_f[:], ctx_t[:, :, bass.ds(g * TG, TG)]).then_inc(ctx_in, 16)

            def stores(g):
                wait_alone(sp, h_hi_ready, g + 1, half_ready, 1)
                sp.dma_start(f(h_hi_all[:, :, bass.ds(g * TG, TG)]), f(h_hi[:])).then_inc(h_kept, 16)
                wait_alone(sp, h_lo_ready, g + 1, half_ready, 1)
                sp.dma_start(f(h_lo_all[:, :, bass.ds(g * TG, TG)]), f(h_lo[:])).then_inc(h_kept, 16)
                wait_alone(sp, cmbt_ready, g + 1, half_ready, 1)
                sp.dma_start(comb[0:NE, bass.ds(g * TG, TG)], comb_t[:]).then_inc(cmb_out, 16)

            loads(0)
            with sp.Fori(0, NG - 1) as g:
                wait_alone(sp, xn_ready, BG * g + BG, half_ready, 1)
                sp.wait_ge(xb_ready, g + 1)
                sp.wait_ge(ctx_hi_ready, g + 1)
                sp.wait_ge(ctx_lo_ready, g + 1)
                loads(g + 1)
                stores(g)
            stores(NG - 1)

            def expert_loads(h, e, slot):
                sp.dma_start(w_raw[:, slot, :], w_exp[bass.ds(e, 1), :, :].rearrange("o p n -> p (o n)")).then_inc(wr_in[slot], 16)

            def combine_loads(h, e, slot):
                row = comb[bass.ds(e, 1), h * CPH * TG:(h + 1) * CPH * TG]
                sp.dma_start(cw[:, slot, :], row.to_broadcast([P, CPH * TG])).then_inc(cw_in[slot], 16)

            def free_slot(E):
                wait_alone(sp, gu_lo, E - 1, half_ready, 1)
                sp.wait_ge(dn_lo, E - 1)
                sp.wait_ge(weighted, CPH * (E - 1))

            for slot in range(2):
                expert_loads(0, slot, slot)
            sp.wait_ge(half_out, 16)
            attention_over(sp)
            for slot in range(2):
                combine_loads(0, slot, slot)
            def pair_loads(h, e):
                for slot in range(2):
                    free_slot(h * NX + e + slot)
                    expert_loads(h, e + slot, slot)
                    combine_loads(h, e + slot, slot)

            def output_stores(h):
                for c in range(CPH):
                    for m in range(KC):
                        sp.wait_ge(y_ready, (h * CPH + c) * KC + m + 1)
                        sp.dma_start(out_t[m * P:(m + 1) * P, (h * CPH + c) * TG:(h * CPH + c + 1) * TG],
                                     y_out[:, c * KC + m, :]).then_inc(y_stored, 16)

            with sp.Fori(1, NX // 2) as q:
                pair_loads(0, 2 * q)
            pair_loads(1, 0)
            output_stores(0)
            with sp.Fori(1, NX // 2) as q:
                pair_loads(1, 2 * q)
            output_stores(1)
            sp.wait_ge(y_stored, 16 * HALVES * 4)

        @block.gpsimd
        def _(pool):
            pool.memset(half_rows[:], 0.5).then_inc(half_ready, 1)
            pool.memset(pad_f[:, :, :, 0:1], 1.0).then_inc(v_pad, 1)
            pool.memset(pad_f[:, :, :, 1:2], 0.0).then_inc(v_pad, 1)
            pool.wait_ge(v_pad, 2)
            pool.tensor_copy(v_hi[:, :, :, DH:VW], pad_f[:]).then_inc(v_pad, 1)
            pool.tensor_copy(v_lo[:, :, :, DH:VW], pad_f[:, :, :, 1:2].to_broadcast([S, BG, NH, 2])).then_inc(v_pad, 1)
            pool.wait_ge(const_in, 16)
            pool.wait_ge(bias_in, 48)
            with pool.Fori(0, NG) as g:
                pool.wait_ge(ctx_hi_ready, g + 1)
                pool.tensor_tensor(ctx_lo[:], ctx_f[:], f(ctx_hi[:]), ALU.subtract).then_inc(ctx_lo_ready, 1)
                pool.wait_ge(var_ready, g + 1)
                pool.tensor_tensor(rstd[:], ve[:], minus_half, ALU.pow).then_inc(rstd_ready, 1)
                pool.wait_ge(x_in, 16 * (g + 1))
                pool.tensor_tensor(xb[:], x_g[:], rb_vo[:, 1, :].unsqueeze(1).to_broadcast([S, BG, D]), ALU.add).then_inc(xb_ready, 1)
                for i in range(2):
                    b = slice(2 * i, 2 * i + 2)
                    pool.wait_ge(v_hi_ready, 2 * g + i + 1)
                    pool.tensor_tensor(v_lo[:, b, :, 0:DH], vf[:, b, :].rearrange("p b (h d) -> p b h d", d=DH),
                                       f(v_hi[:, b, :, 0:DH]), ALU.subtract).then_inc(v_lo_ready, 1)
                pool.wait_ge(var2_ready, g + 1)
                pool.tensor_tensor(rstd[:], ve[:], minus_half, ALU.pow).then_inc(rstd2_ready, 1)

            attention_over(pool)
            pool.memset(zero_b[:], 0.0).then_inc(zero_ready, 1)

            def weigh(N, s, E, new_expert):
                if new_expert:
                    pool.wait_ge(cw_in[(s // 2) % 2], 16 * E)
                pool.wait_ge(gated, N + 1)
                pool.tensor_tensor(act[:, s, :], act[:, s, :], cw[:, (s // 2) % 2, (s % 2) * TG:(s % 2 + 1) * TG],
                                   ALU.mult).then_inc(weighted, 1)

            with pool.Fori(0, HALVES * STEPS // 4) as p:
                for s in range(4):
                    weigh(4 * p + s, s, p + 1, s % 2 == 0)

        @block.scalar
        def _(a):
            a.wait_ge(const_in, 16)
            a.activation(ident_r[:], cst[0:S, 0:S], ACT.Copy).then_inc(const_cast, 1)
            a.activation(ident_b[:], cst[0:S, 0:S], ACT.Copy).then_inc(const_cast, 1)
            a.activation(mask_b[:], mask_f[0:S, :], ACT.Copy).then_inc(const_cast, 1)
            a.wait_ge(weight_in, 32)
            a.activation(wa_hi[:], wa[:], ACT.Copy).then_inc(w_hi_ready, 1)
            a.activation(wg_hi[:], wg[:], ACT.Copy).then_inc(w_hi_ready, 1)
            a.wait_ge(bias_in, 48)

            def prologue(g):
                a.wait_ge(ctx_in, 16 * (g + 1))
                a.activation(ctx_hi[:], ctx_f[:], ACT.Copy).then_inc(ctx_hi_ready, 1)
                for m in range(KC):
                    a.wait_ge(k_psum, KC * g + m + 1)
                    a.activation(k_hi[:, m, :], ps[:, 2 + m, 0:TG], ACT.Identity,
                                 bias=cb_qk[:, 1, m:m + 1]).then_inc(k_hi_ready, 1)
                for i in range(2):
                    b = slice(2 * i, 2 * i + 2)
                    a.wait_ge(vf_ready, 2 * g + i + 1)
                    a.activation(v_hi[:, b, :, 0:DH], vf[:, b, :].rearrange("p b (h d) -> p b h d", d=DH),
                                 ACT.Copy).then_inc(v_hi_ready, 1)
                a.wait_ge(xt_psum, g + 1)
                a.activation(xt_hi[:], ps[:, 0:KC, 0:TG], ACT.Copy).then_inc(xt_hi_ready, 1)
                for m in range(KC):
                    a.wait_ge(q_psum, KC * g + m + 1)
                    a.activation(qf[:, m, :], ps[:, 6 + m, 0:TG], ACT.Identity,
                                 bias=cb_qk[:, 0, m:m + 1]).then_inc(qf_ready, 1)

            def exps(g, j):
                a.wait_ge(shifted, BG * g + j + 1)
                a.activation(prob[:, j % 2, :].rearrange("p (r n) -> p r n", r=PAIRS), ps[0:S, 0:PAIRS, 0:TG], ACT.Exp,
                             scale=DH ** -0.5).then_inc(prob_ready, 1)

            def attention(g):
                exps(g, 0)
                for j in range(BG):
                    B = BG * g + j
                    for r in range(PAIRS):
                        a.wait_ge(pt_psum, PAIRS * B + r + 1)
                        a.activation(pt_hi[:, r % 2, :], ps[0:S, 4 + r % 2, 0:TG], ACT.Copy).then_inc(pt_hi_ready, 1)
                    if j + 1 < BG:
                        exps(g, j + 1)
                    a.wait_ge(ot_psum, B + 1)
                    a.activation(ot_hi[:], ps[:, 7, 0:KC * S].rearrange("p (k q) -> p k q", k=KC),
                                 ACT.Copy).then_inc(ot_hi_ready, 1)

            def epilogue(g):
                a.wait_ge(ht_psum, g + 1)
                a.wait_ge(h_kept, 32 * g + 1)
                a.activation(h_hi[:], ps[:, 0:KC, 0:TG], ACT.Copy).then_inc(h_hi_ready, 1)
                a.wait_ge(x1t_psum, g + 1)
                a.activation(x1t_all[:, :, bass.ds(g * TG, TG)], ps[:, 2:2 + KC, 0:TG], ACT.Copy).then_inc(x1t_ready, 1)
                a.wait_ge(logit_psum, g + 1)
                a.activation(rt[:, 0, :], ps[0:S, 4, 0:BG * NE], ACT.Tanh, scale=0.5).then_inc(tanh_ready, 1)
                a.wait_ge(cmbt_psum, g + 1)
                a.wait_ge(cmb_out, 16 * g + 1)
                a.activation(comb_t[:], ps[0:NE, 5, 0:TG], ACT.Copy).then_inc(cmbt_ready, 1)

            with a.Fori(0, NG) as g:
                prologue(g)
                attention(g)
                epilogue(g)

            def split_gu(loaded, slot):
                a.wait_ge(wr_in[slot], 16 * loaded)
                a.activation(w_hi[:, slot, 0:2 * D], w_raw[:, slot, 0:2 * D], ACT.Copy).then_inc(gu_hi, 1)

            def split_dn(slot):
                a.activation(w_hi[:, slot, 2 * D:], w_raw[:, slot, 2 * D:], ACT.Copy).then_inc(dn_hi, 1)

            def lead(N, s, pair):
                a.wait_ge(gu_psum, N + 1)
                a.activation(act[:, s, :], ps[:, 4 + 2 * (s % 2), 0:TG], ACT.Tanh, scale=0.5).then_inc(tanh_e, 1)

            def split(N, s, pair):
                if s % 2 == 1:
                    split_dn(s // 2)
                elif not (isinstance(N, int) and N // 2 + 1 >= HALVES * NX):
                    split_gu(pair + 1 + s // 2, (s // 2 + 1) % 2)

            def lag(N, s):
                a.wait_ge(weighted, N + 1)
                a.activation(a_hi[:, s, :], act[:, s, :], ACT.Copy).then_inc(a_hi_ready, 1)

            attention_over(a)
            split_gu(1, 0)
            lead(0, 0, 0)
            split(0, 0, 0)
            total = HALVES * STEPS
            with a.Fori(0, total // 4 - 1) as p:
                for s in range(4):
                    k = 4 * p + s
                    lead(k + 1, (s + 1) % 4, p + (s + 1) // 4)
                    lag(k, s)
                    split(k + 1, (s + 1) % 4, p + (s + 1) // 4)
            for k in range(total - 4, total):
                if k + 1 < total:
                    lead(k + 1, (k + 1) % 4, (k + 1) // 4)
                lag(k, k % 4)
                if k + 1 < total:
                    split(k + 1, (k + 1) % 4, (k + 1) // 4)

        @block.vector
        def _(v):
            v.wait_ge(w_hi_ready, 2)
            v.tensor_tensor(wa_lo[:], wa[:], f(wa_hi[:]), ALU.subtract).then_inc(w_lo_ready, 1)
            v.tensor_tensor(wg_lo[:], wg[:], f(wg_hi[:]), ALU.subtract).then_inc(w_lo_ready, 1)
            v.wait_ge(const_in, 16)
            v.wait_ge(bias_in, 48)
            done = [0]

            def then(g, *instructions, plain=False):
                for i in instructions:
                    i.then_inc(step, 1)
                done[0] += len(instructions)
                if plain:
                    wait_alone(v, step, VECTOR_STEPS * g + done[0], const_in, 16)
                else:
                    v.wait_ge(step, VECTOR_STEPS * g + done[0])

            def norm_stats(g, rows, ready):
                then(g, *[v.bn_stats(st[:, j, :], rows[:, j, :]) for j in range(BG)], plain=True)
                then(g, *[v.bn_aggr(mv[:, j, :], st[:, j, :]) for j in range(BG)])
                v.tensor_scalar(ve[:], mv[:, :, 1], EPS, None, ALU.add).then_inc(ready, 1)

            def normalise(out, rows, ready):
                for j in range(BG):
                    v.tensor_scalar(out[:, j, :], rows[:, j, :], mv[:, j, 0:1], rstd[:, j:j + 1],
                                    ALU.subtract, ALU.mult).then_inc(ready, 1)

            def prologue(g):
                v.wait_ge(x_in, 16 * (g + 1))
                norm_stats(g, x_g, var_ready)
                v.wait_ge(rstd_ready, g + 1)
                normalise(xn, x_g, xn_ready)
                for m in range(KC):
                    v.wait_ge(k_hi_ready, KC * g + m + 1)
                    v.scalar_tensor_tensor(k_lo[:, m, :], ps[:, 2 + m, 0:TG], cb_qk[:, 1, m:m + 1], f(k_hi[:, m, :]),
                                           ALU.add, ALU.subtract).then_inc(k_lo_ready, 1)
                for i in range(2):
                    v.wait_ge(v_psum, 2 * g + i + 1)
                    v.tensor_tensor(vf[:, 2 * i:2 * i + 2, :], ps[0:S, 4 + i, :].rearrange("p (b d) -> p b d", b=2),
                                    rb_vo[:, 0, :].unsqueeze(1).to_broadcast([S, 2, D]), ALU.add).then_inc(vf_ready, 1)
                v.wait_ge(xt_hi_ready, g + 1)
                v.tensor_tensor(xt_lo[:], ps[:, 0:KC, 0:TG], f(xt_hi[:]), ALU.subtract).then_inc(xt_lo_ready, 1)
                v.wait_ge(qf_ready, KC * (g + 1))
                then(g, *[v.tensor_scalar(q_hi[i][:], qf[:], pair_mask[:, i:i + 1], None, ALU.mult) for i in range(2)])
                for i in range(2):
                    v.scalar_tensor_tensor(q_lo[i][:], qf[:], pair_mask[:, i:i + 1], f(q_hi[i][:]),
                                           ALU.mult, ALU.subtract).then_inc(q_ready, 1)

            def maxima(g, j):
                v.wait_ge(score_psum, BG * g + j + 1)
                then(g, v.tensor_reduce(nm[:].rearrange("p (r n) -> p r n", r=PAIRS),
                                        ps[0:S, 0:PAIRS, 0:TG].rearrange("p r (n k) -> p r n k", k=S), AX.X, ALU.max,
                                        negate=True))
                then(g, v.tensor_copy(nm_hi[:], nm[:]))
                v.tensor_tensor(nm_lo[:], nm[:], f(nm_hi[:]), ALU.subtract).then_inc(nm_ready, 1)

            def residual(g, j):
                B = BG * g + j
                v.wait_ge(xb_ready, g + 1)
                v.wait_ge(proj_psum, B + 1)
                v.tensor_tensor(x1[:, j, :], ps[0:S, 7, D:2 * D], xb[:, j, :], ALU.add).then_inc(x1_ready, 1)

            def attention(g):
                maxima(g, 0)
                for j in range(BG):
                    B = BG * g + j
                    for r in range(PAIRS):
                        v.wait_ge(pt_hi_ready, PAIRS * B + r + 1)
                        v.tensor_tensor(pt_lo[:, r % 2, :], ps[0:S, 4 + r % 2, 0:TG], f(pt_hi[:, r % 2, :]),
                                        ALU.subtract).then_inc(pt_lo_ready, 1)
                        if r == 1 and j > 0:
                            residual(g, j - 1)
                    if j + 1 < BG:
                        maxima(g, j + 1)
                    v.wait_ge(pv_quarter, PAIRS * (B + 1))
                    o = ps[0:S, 6, 0:NH * VW].rearrange("p (h d) -> p h d", d=VW)
                    then(g, v.reciprocal(rden[:], o[:, :, DH]))
                    v.tensor_tensor(on[:].rearrange("p (h d) -> p h d", d=DH), o[:, :, 0:DH],
                                    rden[:].unsqueeze(2).to_broadcast([S, NH, DH]), ALU.mult).then_inc(on_ready, 1)
                    v.wait_ge(ot_hi_ready, B + 1)
                    v.tensor_tensor(ot_lo[:], ps[:, 7, 0:KC * S].rearrange("p (k q) -> p k q", k=KC), f(ot_hi[:]),
                                    ALU.subtract).then_inc(ot_lo_ready, 1)
                residual(g, BG - 1)

            def route(g):
                R = lambda i: rt[:, i, :]
                by_group = lambda ap: ap.rearrange("p (n e) -> p n e", e=EPG)
                v.wait_ge(tanh_ready, g + 1)
                then(g, v.tensor_scalar(R(1), R(0), 0.5, 0.5, ALU.mult, ALU.add))
                then(g, v.tensor_tensor(R(2).rearrange("p (b e) -> p b e", e=NE), R(1).rearrange("p (b e) -> p b e", e=NE),
                                        gb[:].unsqueeze(1).to_broadcast([S, BG, NE]), ALU.add))
                pairs = R(2).rearrange("p (n t) -> p n t", t=2)
                then(g, v.tensor_tensor(pair_max[:].rearrange("p n t -> p (n t)"), pairs[:, :, 0], pairs[:, :, 1], ALU.max),
                     v.tensor_tensor(pair_min[:].rearrange("p n t -> p (n t)"), pairs[:, :, 0], pairs[:, :, 1], ALU.min))
                then(g, v.tensor_tensor(gs[:, 0, :], pair_max[:, :, 0], pair_max[:, :, 1], ALU.max),
                     v.tensor_tensor(gs[:, 1, :], pair_max[:, :, 0], pair_max[:, :, 1], ALU.min),
                     v.tensor_tensor(gs[:, 2, :], pair_min[:, :, 0], pair_min[:, :, 1], ALU.max))
                then(g, v.tensor_tensor(gs[:, 1, :], gs[:, 1, :], gs[:, 2, :], ALU.max))
                then(g, v.tensor_tensor(gs[:, 0, :], gs[:, 0, :], gs[:, 1, :], ALU.add))
                score = gs[:, 0, :].rearrange("p (b n) -> p b n", n=NGRP)
                own = score.unsqueeze(3).to_broadcast([S, BG, NGRP, NGRP])
                other = score.unsqueeze(2).to_broadcast([S, BG, NGRP, NGRP])
                flat = lambda ap: ap.rearrange("p b n m -> p b (n m)")
                then(g, v.tensor_tensor(cmpa[:], other, own, ALU.is_gt), v.tensor_tensor(cmpb[:], other, own, ALU.is_equal))
                then(g, v.tensor_tensor(flat(cmpb[:]), flat(cmpb[:]), earlier.unsqueeze(1).to_broadcast([S, BG, NGRP * NGRP]), ALU.mult))
                then(g, v.tensor_tensor(cmpa[:], cmpa[:], cmpb[:], ALU.add))
                then(g, v.tensor_reduce(gs[:, 2, :].rearrange("p (b n) -> p b n", n=NGRP), cmpa[:], AX.X, ALU.add))
                then(g, v.tensor_scalar(gs[:, 3, :], gs[:, 2, :], float(TOPG), None, ALU.is_lt))
                then(g, v.tensor_tensor(by_group(R(3)), by_group(R(2)),
                                        gs[:, 3, :].unsqueeze(2).to_broadcast([S, BG * NGRP, EPG]), ALU.mult), plain=True)
                part_of = lambda i, b: rt[:, i, b * NE:(b + 1) * NE]
                then(g, *[v.max(best[:, b, :], part_of(3, b)) for b in range(BG)], plain=True)
                then(g, *[v.match_replace(part_of(4, b), best[:, b, :], part_of(3, b), TAKEN) for b in range(BG)])
                then(g, v.tensor_tensor(R(5), R(4), R(3), ALU.not_equal))
                then(g, v.tensor_tensor(R(6), R(5), R(1), ALU.mult))
                then(g, v.tensor_reduce(wsum[:, 0, :], R(6).rearrange("p (b e) -> p b e", e=NE), AX.X, ALU.add))
                then(g, v.tensor_scalar(wsum[:, 1, :], wsum[:, 0, :], 1e-20, None, ALU.add))
                then(g, v.reciprocal(wsum[:, 0, :], wsum[:, 1, :]))
                v.scalar_tensor_tensor(R(7).rearrange("p (b e) -> p b e", e=NE), R(6).rearrange("p (b e) -> p b e", e=NE),
                                       ROUTE_SCALE / 2, wsum[:, 0, :].unsqueeze(2).to_broadcast([S, BG, NE]),
                                       ALU.mult, ALU.mult).then_inc(cmb_ready, 1)

            def epilogue(g):
                v.wait_ge(x1_ready, BG * (g + 1))
                norm_stats(g, x1, var2_ready)
                v.wait_ge(rstd2_ready, g + 1)
                normalise(h1, x1, h1_ready)
                v.wait_ge(h_kept, 32 * g + 1)
                v.wait_ge(h_hi_ready, g + 1)
                v.tensor_tensor(h_lo[:], ps[:, 0:KC, 0:TG], f(h_hi[:]), ALU.subtract).then_inc(h_lo_ready, 1)
                route(g)

            with v.Fori(0, NG) as g:
                prologue(g)
                attention(g)
                epilogue(g)
            assert done[0] == VECTOR_STEPS, done

            def split_gu(count, slot):
                v.wait_ge(gu_hi, count)
                v.tensor_tensor(w_lo[:, slot, 0:2 * D], w_raw[:, slot, 0:2 * D], f(w_hi[:, slot, 0:2 * D]),
                                ALU.subtract).then_inc(gu_lo, 1)

            def lead(N, s):
                v.wait_ge(tanh_e, N + 1)
                v.scalar_tensor_tensor(act[:, s, :], act[:, s, :], 1.0, ps[:, 4 + 2 * (s % 2), 0:TG], ALU.add,
                                       ALU.mult).then_inc(opened, 1)
                v.wait_ge(opened, N + 1)
                v.tensor_tensor(act[:, s, :], act[:, s, :], ps[:, 5 + 2 * (s % 2), 0:TG], ALU.mult).then_inc(gated, 1)

            def split_at(pair, s, last=False):
                if s % 2 == 1:
                    slot = s // 2
                    v.wait_ge(dn_hi, 2 * pair + slot + 1)
                    v.tensor_tensor(w_lo[:, slot, 2 * D:], w_raw[:, slot, 2 * D:], f(w_hi[:, slot, 2 * D:]),
                                    ALU.subtract).then_inc(dn_lo, 1)
                elif not last:
                    split_gu(2 * pair + s // 2 + 2, (s // 2 + 1) % 2)

            def lag(N, s):
                v.wait_ge(a_hi_ready, N + 1)
                v.tensor_tensor(a_lo[:, s, :], act[:, s, :], f(a_hi[:, s, :]), ALU.subtract).then_inc(a_lo_ready, 1)

            def outputs(h):
                v.wait_ge(down_done, STEPS * (h + 1))
                for c in range(CPH):
                    for m in range(KC):
                        if h:
                            v.wait_ge(y_stored, 16 * (c * KC + m + 1))
                        v.tensor_tensor(y_out[:, c * KC + m, :], ps[:, c * KC + m, 0:TG],
                                        x1t_all[:, m, (h * CPH + c) * TG:(h * CPH + c + 1) * TG],
                                        ALU.add).then_inc(y_ready, 1)

            attention_over(v)
            split_gu(1, 0)
            lead(0, 0)
            split_at(0, 0)
            total = HALVES * STEPS
            for h in range(HALVES):
                with v.Fori(h * STEPS // 4, (h + 1) * STEPS // 4 - (1 if h else 0)) as p:
                    for s in range(4):
                        k = 4 * p + s
                        lead(k + 1, (s + 1) % 4)
                        lag(k, s)
                        split_at(p + (s + 1) // 4, (s + 1) % 4)
                if h == 0:
                    outputs(0)
            for k in range(total - 4, total):
                if k + 1 < total:
                    lead(k + 1, (k + 1) % 4)
                lag(k, k % 4)
                if k + 1 < total:
                    split_at((k + 1) // 4, (k + 1) % 4, last=(k + 1) // 2 + 1 >= HALVES * NX)
            outputs(1)

        @block.tensor
        def _(t):
            def product(out, pairs):
                n = 3 * len(pairs)
                i = 0
                for w_h, w_l, m_h, m_l in pairs:
                    for w, m in ((w_h, m_h), (w_h, m_l), (w_l, m_h)):
                        last = t.matmul(out, w, m, start=(i == 0), stop=(i == n - 1))
                        i += 1
                return last

            def prologue(g):
                t.wait_ge(ctx_hi_ready, g + 1)
                t.wait_ge(ctx_lo_ready, g + 1)
                for m in range(KC):
                    w = lambda a, k: a[:, 1, k, m * P:(m + 1) * P]
                    product(ps[:, 2 + m, 0:TG], [(w(wa_hi, k), w(wa_lo, k), ctx_hi[:, k, :], ctx_lo[:, k, :])
                                                 for k in range(KC)]).then_inc(k_psum, 1)
                for j in range(BG):
                    c = lambda a, k: a[:, k, j * S:(j + 1) * S]
                    last = product(ps[0:S, 4 + j // 2, (j % 2) * D:(j % 2 + 1) * D],
                                   [(c(ctx_hi, k), c(ctx_lo, k), wa_hi[:, 2, k, :], wa_lo[:, 2, k, :]) for k in range(KC)])
                    if j % 2:
                        last.then_inc(v_psum, 1)
                t.wait_ge(xn_ready, BG * (g + 1))
                for k in range(KC):
                    for j in range(BG):
                        last = t.transpose(ps[:, k, j * S:(j + 1) * S], xn[:, j, k * P:(k + 1) * P], ident[0:S, 0:S])
                last.then_inc(xt_psum, 1)
                t.wait_ge(xt_hi_ready, g + 1)
                t.wait_ge(xt_lo_ready, g + 1)
                for m in range(KC):
                    w = lambda a, k: a[:, 0, k, m * P:(m + 1) * P]
                    product(ps[:, 6 + m, 0:TG], [(w(wa_hi, k), w(wa_lo, k), xt_hi[:, k, :], xt_lo[:, k, :])
                                                 for k in range(KC)]).then_inc(q_psum, 1)

            def scores(j, r):
                t.matmul(ps[0:S, r, 0:TG], ident_b[:], mask_b[:], start=True, stop=False, skip_group_check=True)
                rows = slice(32 * r, 32 * r + 32)
                cols = slice(j * S, (j + 1) * S)
                for n in range(4):
                    m, i = n // 2, n % 2
                    for q, kk in ((q_hi[i], k_hi), (q_hi[i], k_lo), (q_lo[i], k_hi)):
                        last = t.matmul(ps[0:S, r, n * S:(n + 1) * S], q[rows, m, cols], kk[rows, m, cols],
                                        start=False, stop=False, skip_group_check=True)
                return last

            def shift(g, j):
                t.wait_ge(nm_ready, BG * g + j + 1)
                for r in range(PAIRS):
                    for part_of in (nm_hi, nm_lo):
                        last = t.matmul(ps[0:S, r, 0:TG], ident_r[:],
                                        part_of[:, 4 * r:4 * r + 4].unsqueeze(2).to_broadcast([S, 4, S]),
                                        start=False, stop=part_of is nm_lo, skip_group_check=True)
                last.then_inc(shifted, 1)

            def turn(j, r):
                for n in range(4):
                    last = t.transpose(ps[0:S, 4 + r % 2, n * S:(n + 1) * S],
                                       prob[:, j % 2, (4 * r + n) * S:(4 * r + n + 1) * S], ident[0:S, 0:S])
                last.then_inc(pt_psum, 1)

            def values(g, j, r):
                B = BG * g + j
                t.wait_ge(pt_hi_ready, PAIRS * B + r + 1)
                t.wait_ge(pt_lo_ready, PAIRS * B + r + 1)
                for n in range(4):
                    h = 8 * (n // 2) + 2 * r + n % 2
                    c = slice(n * S, (n + 1) * S)
                    last = product(ps[0:S, 6, h * VW:(h + 1) * VW],
                                   [(pt_hi[:, r % 2, c], pt_lo[:, r % 2, c], v_hi[:, j, h, :], v_lo[:, j, h, :])])
                last.then_inc(pv_quarter, 1)

            def project(g, j):
                B = BG * g + j
                t.wait_ge(ot_hi_ready, B + 1)
                t.wait_ge(ot_lo_ready, B + 1)
                product(ps[0:S, 7, D:2 * D], [(ot_hi[:, k, :], ot_lo[:, k, :], wa_hi[:, 3, k, :], wa_lo[:, 3, k, :])
                                              for k in range(KC)]).then_inc(proj_psum, 1)

            def attention(g):
                t.wait_ge(k_hi_ready, KC * (g + 1))
                t.wait_ge(k_lo_ready, KC * (g + 1))
                t.wait_ge(q_ready, 2 * (g + 1))
                for r in range(PAIRS):
                    last = scores(0, r)
                last.then_inc(score_psum, 1)
                shift(g, 0)
                t.wait_ge(v_hi_ready, 2 * (g + 1))
                t.wait_ge(v_lo_ready, 2 * (g + 1))
                for j in range(BG):
                    t.wait_ge(prob_ready, BG * g + j + 1)
                    turn(j, 0)
                    for r in range(PAIRS):
                        if r + 1 < PAIRS:
                            turn(j, r + 1)
                        if j + 1 < BG:
                            last = scores(j + 1, r)
                            if r == PAIRS - 1:
                                last.then_inc(score_psum, 1)
                        values(g, j, r)
                        if r == 0 and j > 0:
                            project(g, j - 1)
                    if j + 1 < BG:
                        shift(g, j + 1)
                    if j > 0:
                        t.wait_ge(x1_ready, BG * g + j)
                    t.wait_ge(on_ready, BG * g + j + 1)
                    for k in range(KC):
                        last = t.transpose(ps[:, 7, k * S:(k + 1) * S], on[:, k * P:(k + 1) * P], ident[0:S, 0:S])
                    last.then_inc(ot_psum, 1)
                project(g, BG - 1)

            def epilogue(g):
                for rows, ready, bank, done in ((x1, x1_ready, 2, x1t_psum), (h1, h1_ready, 0, ht_psum)):
                    t.wait_ge(ready, BG * (g + 1))
                    for k in range(KC):
                        for j in range(BG):
                            last = t.transpose(ps[:, bank + k, j * S:(j + 1) * S], rows[:, j, k * P:(k + 1) * P],
                                               ident[0:S, 0:S])
                    last.then_inc(done, 1)
                t.wait_ge(h_hi_ready, g + 1)
                t.wait_ge(h_lo_ready, g + 1)
                for j in range(BG):
                    c = lambda a, k: a[:, k, j * S:(j + 1) * S]
                    last = product(ps[0:S, 4, j * NE:(j + 1) * NE],
                                   [(c(h_hi, k), c(h_lo, k), wg_hi[:, k, :], wg_lo[:, k, :]) for k in range(KC)])
                last.then_inc(logit_psum, 1)
                t.wait_ge(x1t_ready, g + 1)
                t.wait_ge(cmb_ready, g + 1)
                for j in range(BG):
                    last = t.transpose(ps[0:NE, 5, j * S:(j + 1) * S], rt[:, 7, j * NE:(j + 1) * NE], ident[0:S, 0:S])
                last.then_inc(cmbt_psum, 1)
                t.wait_ge(cmbt_ready, g + 1)

            t.wait_ge(const_in, 16)
            t.wait_ge(const_cast, 3)
            t.wait_ge(w_lo_ready, 2)
            t.wait_ge(v_pad, 4)
            with t.Fori(0, NG) as g:
                prologue(g)
                attention(g)
                epilogue(g)

            def gate_up(N, s, col, experts):
                slot = s // 2
                if s % 2 == 0:
                    t.wait_ge(gu_hi, experts)
                    t.wait_ge(gu_lo, experts)
                if not (isinstance(N, int) and N < 2):
                    t.wait_ge(gated, N - 1)
                for part_of in range(2):
                    w = lambda a, k: a[:, slot, (2 * part_of + k) * P:(2 * part_of + k + 1) * P]
                    last = product(ps[:, 4 + 2 * (s % 2) + part_of, 0:TG],
                                   [(w(w_hi, k), w(w_lo, k), h_hi_all[:, k, col:col + TG], h_lo_all[:, k, col:col + TG])
                                    for k in range(KC)])
                last.then_inc(gu_psum, 1)

            def down(k, s, experts):
                slot = s // 2
                if s % 2 == 0:
                    t.wait_ge(dn_hi, experts)
                    t.wait_ge(dn_lo, experts)
                t.wait_ge(a_hi_ready, k + 1)
                t.wait_ge(a_lo_ready, k + 1)
                for m in range(KC):
                    w = lambda a: a[:, slot, 2 * D + m * P:2 * D + (m + 1) * P]
                    for i, (ww, mm) in enumerate(((w_hi, a_hi), (w_hi, a_lo), (w_lo, a_hi))):
                        last = t.matmul(ps[:, (s % 2) * KC + m, 0:TG], w(ww), mm[:, s, :], start=False, stop=False,
                                        skip_group_check=True)
                last.then_inc(down_done, 1)

            t.wait_ge(h_kept, 32 * NG + 1)
            gate_up(0, 0, 0, 1)
            gate_up(1, 1, TG, 1)
            total = HALVES * STEPS
            for h in range(HALVES):
                t.wait_ge(zero_ready, 1)
                if h:
                    t.wait_ge(y_ready, 4)
                for b in range(CPH * KC):
                    t.matmul(ps[:, b, 0:TG], zero_b[:, 0:P], zero_b[:], start=True, stop=False, skip_group_check=True)
                col = lambda c, later: ((h + later) * CPH + c) * TG

                with t.Fori(h * STEPS // 4, (h + 1) * STEPS // 4 - 1) as p:
                    for s in range(4):
                        gate_up(4 * p + s + 2, (s + 2) % 4, col(s % 2, 0), 2 * p + s // 2 + 2)
                        down(4 * p + s, s, 2 * p + s // 2 + 1)
                for s in range(4):
                    N = (h + 1) * STEPS - 4 + s
                    if N + 2 < total:
                        gate_up(N + 2, (s + 2) % 4, col(s % 2, 1 if s >= 2 else 0), N // 2 + 2)
                    down(N, s, N // 2 + 1)


def constants():
    import numpy as np
    cst = np.zeros((P, CST), np.float32)
    cst[:, 0:P] = np.eye(P)
    causal = np.where(np.arange(S)[None, :] <= np.arange(S)[:, None], 0.0, MASKED)
    cst[0:S, P:P + TG] = np.tile(causal, (1, 4))
    parity = (np.arange(P) // DH) % 2
    cst[:, P + TG] = parity == 0
    cst[:, P + TG + 1] = parity == 1
    g = np.arange(NGRP)
    cst[:, P + TG + 2:P + TG + 2 + NGRP * NGRP] = (g[None, :] < g[:, None]).reshape(1, -1)
    cst[:, -BG:] = -0.5
    return cst


def kernel(x, ctx_1024, L0_xattn_Wq, L0_xattn_bq, L0_xattn_Wk, L0_xattn_bk, L0_xattn_Wv, L0_xattn_bv, L0_xattn_Wo,
           L0_xattn_bo, L0_ffn_gate_w, L0_ffn_gate_bias, L0_ffn_w_gate, L0_ffn_w_up, L0_ffn_w_down, L0_ffn_sh_gate,
           L0_ffn_sh_up, L0_ffn_sh_down):
    import numpy as np
    import concourse.bacc as bacc
    from concourse.bass_utils import run_bass_kernel_spmd

    A = np.asarray
    rows = lambda w: A(w).reshape(KC, P, -1).transpose(1, 0, 2)
    turned = lambda w: A(w).transpose(0, 2, 1)
    gate = np.concatenate([turned(L0_ffn_w_gate), turned(A(L0_ffn_sh_gate).reshape(2, FI, D))])
    up = np.concatenate([turned(L0_ffn_w_up), turned(A(L0_ffn_sh_up).reshape(2, FI, D))])
    down = np.concatenate([turned(L0_ffn_w_down), A(L0_ffn_sh_down).T.reshape(2, FI, D)])
    by_chunk = lambda w: w.reshape(NX, KC, P, FI).transpose(0, 2, 1, 3).reshape(NX, P, KC * FI)
    arrays = {
        "x": A(x).transpose(1, 0, 2),
        "ctx_t": A(ctx_1024)[:, :S].transpose(2, 0, 1).reshape(KC, P, T).transpose(1, 0, 2),
        "w_attn": np.stack([rows(w) for w in (L0_xattn_Wq, L0_xattn_Wk, L0_xattn_Wv, L0_xattn_Wo)], 1),
        "w_gate_t": rows(A(L0_ffn_gate_w).T),
        "col_bias": np.stack([A(b).reshape(KC, P).T for b in (L0_xattn_bq, L0_xattn_bk)], 1),
        "row_bias": np.stack([A(L0_xattn_bv), A(L0_xattn_bo)]),
        "gate_bias": A(L0_ffn_gate_bias),
        "w_exp": np.concatenate([by_chunk(gate), by_chunk(up), down], 2),
        "consts": constants(),
    }
    arrays = {k: np.ascontiguousarray(a) for k, a in arrays.items()}
    nc = bacc.Bacc("TRN2", target_bir_lowering=False, num_devices=1)
    args = [nc.dram_tensor(k, a.shape, mybir.dt.from_np(a.dtype), kind="ExternalInput").ap() for k, a in arrays.items()]
    out_t = nc.dram_tensor("out_t", (D, T), F32, kind="ExternalOutput").ap()
    block_kernel(nc, *args, out_t)
    r = run_bass_kernel_spmd(nc, [arrays], core_ids=[0])
    return np.ascontiguousarray(r.results[0]["out_t"].T).reshape(NB, S, D)
```

```python
from contextlib import ExitStack

import concourse.bass as bass
from concourse import mybir

ALU = mybir.AluOpType
ACT = mybir.ActivationFunctionType
AX = mybir.AxisListType
F32 = mybir.dt.float32
F32R = mybir.dt.float32r
BF16 = mybir.dt.bfloat16

P = 128
D = 256
KC = D // P
NB = 16
S = 100
NG = 4
BG = NB // NG
TG = BG * S
T = NB * S
NH = 16
DH = D // NH
HC = NH // KC
QUADS = NH // 4
VW = DH + 2
VX = VW + DH
KQ_DMAS = HC + 1
NE = 32
NX = NE + 2
FI = 128
NGRP = 8
EPG = NE // NGRP
TOPG = 4
EPS = 1e-5
ROUTE_SCALE = 2.5
HALVES = 2
CPH = 2
STEPS = NX * CPH
CST = P + TG + NGRP * NGRP + BG
MASKED = -1e30
TAKEN = -3e38
RING = (4, 5, 5, 4)



def block_kernel(nc, x, ctx_t, w_attn, w_gate_t, col_bias, row_bias, gate_bias, w_exp, consts, out_t):
    comb = nc.dram_tensor("combine_rows", (NX, T), F32).ap()

    with ExitStack() as top:
        sem = lambda name: top.enter_context(nc.semaphore(name))
        keep = lambda name, shape, dt=F32: top.enter_context(nc.sbuf_tensor(name, shape, dt))
        ps = top.enter_context(nc.psum_tensor("ps", [P, 8, 512], F32))

        proj_part = ExitStack()
        tmp = lambda name, shape, dt=F32: proj_part.enter_context(nc.sbuf_tensor(name, shape, dt))
        x_g = tmp("x_g", [S, BG, D])
        ctx_f = tmp("ctx_f", [P, KC, TG])
        ctx_hi = tmp("ctx_hi", [P, KC, TG], F32R)
        ctx_lo = tmp("ctx_lo", [P, KC, TG], F32R)
        xn = tmp("xn", [S, BG, D])
        xt_hi = tmp("xt_hi", [P, KC, TG], F32R)
        xt_lo = tmp("xt_lo", [P, KC, TG], F32R)
        st = tmp("st", [S, BG, 6])
        mv = tmp("mv", [S, BG, 2])
        ve = tmp("ve", [S, BG])
        rstd = tmp("rstd", [S, BG])
        proj_part.close()

        x1t_all = keep("x1t_all", [P, KC, T])
        h_hi_all = keep("h_hi_all", [P, KC, T], F32R)
        h_lo_all = keep("h_lo_all", [P, KC, T], F32R)
        w_raw = keep("w_raw", [P, 2, 3 * D])

        part = ExitStack()
        tmp = lambda name, shape, dt=F32: part.enter_context(nc.sbuf_tensor(name, shape, dt))
        cst = tmp("cst", [P, CST])
        ident = cst[:, 0:128]
        mask_f = cst[:, 128:128 + TG]
        earlier = cst[0:S, 528:592]
        minus_half = cst[0:S, 592:596]
        ident_r = tmp("ident_r", [S, S], F32R)
        ident_b = tmp("ident_b", [S, S], BF16)
        mask_b = tmp("mask_b", [S, TG], BF16)
        wa = tmp("wa", [P, 4, KC, D])
        wa_hi = tmp("wa_hi", [P, 4, KC, D], F32R)
        wa_lo = tmp("wa_lo", [P, 4, KC, D], F32R)
        wg = tmp("wg", [P, KC, NE])
        wg_hi = tmp("wg_hi", [P, KC, NE], F32R)
        wg_lo = tmp("wg_lo", [P, KC, NE], F32R)
        cb_qk = tmp("cb_qk", [P, 2, KC])
        rb_vo = tmp("rb_vo", [S, 2, D])
        gb = tmp("gb", [S, NE])
        half_rows = tmp("half_rows", [2, T])
        q_all = tmp("q_all", [P, 2, KC, T], F32R)
        k_all = tmp("k_all", [P, 2, KC, T], F32R)
        q_hi_all, q_lo_all = q_all[:, 0], q_all[:, 1]
        k_hi_all, k_lo_all = k_all[:, 0], k_all[:, 1]
        v_all = tmp("v_all", [S, NB, D])
        pass_part = ExitStack()
        loop = lambda name, shape, dt=F32: pass_part.enter_context(nc.sbuf_tensor(name, shape, dt))
        k_blocks = loop("k_blocks", [P, 2, 2, KC, HC, S], F32R)
        q_now = loop("q_now", [P, 2, 2, KC, S], F32R)
        v_s = loop("v_s", [S, 2, NH, VX], F32R)
        pad_f = loop("pad_f", [S, 2, NH, 2])
        nm = loop("nm", [S, NH])
        nm_hi = loop("nm_hi", [S, NH], F32R)
        nm_lo = loop("nm_lo", [S, NH], F32R)
        prob = loop("prob", [S, NH * S])
        pt_hi = loop("pt_hi", [S, 2, 4 * S], F32R)
        pt_lo = loop("pt_lo", [S, 2, 4 * S], F32R)
        rden = loop("rden", [S, NH])
        o_sum = loop("o_sum", [S, NH, DH])
        on = loop("on", [S, D])
        ot_hi = loop("ot_hi", [P, KC, S], F32R)
        ot_lo = loop("ot_lo", [P, KC, S], F32R)
        x_r = loop("x_r", [S, 4, D])
        x1 = loop("x1", [S, 2, D])
        h1 = loop("h1", [S, 2, D])
        st2 = loop("st2", [S, 6])
        mv2 = loop("mv2", [S, 2])
        ve2 = loop("ve2", [S, 1])
        rstd2 = loop("rstd2", [S, 1])
        pass_part.close()
        logit_t = tmp("logit_t", [NE, T])
        rt = tmp("rt", [S, 8, NB * NE])
        pair_max = tmp("pair_max", [S, NB * NGRP, 2])
        pair_min = tmp("pair_min", [S, NB * NGRP, 2])
        gs = tmp("gs", [S, 4, NB * NGRP])
        cmpa = tmp("cmpa", [S, NB, NGRP, NGRP])
        cmpb = tmp("cmpb", [S, NB, NGRP, NGRP])
        best = tmp("best", [S, NB, 8])
        wsum = tmp("wsum", [S, 2, NB])
        comb_t = tmp("comb_t", [NE, T])
        part.close()

        w_hi = keep("w_hi", [P, 2, 3 * D], F32R)
        w_lo = keep("w_lo", [P, 2, 3 * D], F32R)
        cw = keep("cw", [P, 2, CPH * TG])
        act = keep("act", [P, 4, TG])
        a_hi = keep("a_hi", [P, 4, TG], F32R)
        a_lo = keep("a_lo", [P, 4, TG], F32R)
        y_out = keep("y_out", [P, 4, TG])
        zero_b = keep("zero_b", [P, TG], BF16)

        const_in = sem("const_in"); weight_in = sem("weight_in"); bias_in = sem("bias_in")
        const_cast = sem("const_cast"); w_hi_ready = sem("w_hi_ready"); w_lo_ready = sem("w_lo_ready")
        v_pad = sem("v_pad"); blocks_zeroed = sem("blocks_zeroed"); half_ready = sem("half_ready"); half_out = sem("half_out")
        x_in = sem("x_in"); ctx_in = sem("ctx_in")
        st_done = sem("st_done"); mv_done = sem("mv_done"); var_ready = sem("var_ready")
        rstd_ready = sem("rstd_ready"); xn_ready = sem("xn_ready")
        ctx_hi_ready = sem("ctx_hi_ready"); ctx_lo_ready = sem("ctx_lo_ready")
        k_psum = sem("k_psum"); k_hi_ready = sem("k_hi_ready"); k_lo_ready = sem("k_lo_ready")
        xt_psum = sem("xt_psum"); xt_hi_ready = sem("xt_hi_ready"); xt_lo_ready = sem("xt_lo_ready")
        v_psum = sem("v_psum"); v_ready = sem("v_ready")
        q_psum = sem("q_psum"); q_hi_ready = sem("q_hi_ready"); q_lo_ready = sem("q_lo_ready")
        kq_in = [sem(f"kq_in{i}") for i in range(2)]; xr_in = [sem(f"xr_in{i}") for i in range(4)]
        xr_ready = sem("xr_ready"); v_hi_ready = sem("v_hi_ready"); v_lo_ready = sem("v_lo_ready")
        score_psum = sem("score_psum"); max_ready = sem("max_ready"); nm_hi_ready = sem("nm_hi_ready"); nm_ready = sem("nm_ready")
        shifted = sem("shifted"); prob_ready = sem("prob_ready")
        pt_psum = sem("pt_psum"); pt_hi_ready = sem("pt_hi_ready"); pt_lo_ready = sem("pt_lo_ready")
        pv_psum = sem("pv_psum"); o_read = sem("o_read"); on_ready = sem("on_ready")
        ot_psum = sem("ot_psum"); ot_hi_ready = sem("ot_hi_ready"); ot_lo_ready = sem("ot_lo_ready")
        proj_psum = sem("proj_psum"); x1_ready = sem("x1_ready")
        st2_done = sem("st2_done"); mv2_done = sem("mv2_done"); var2_ready = sem("var2_ready")
        rstd2_ready = sem("rstd2_ready"); h1_ready = sem("h1_ready")
        ht_psum = sem("ht_psum"); h_hi_ready = sem("h_hi_ready"); h_lo_ready = sem("h_lo_ready"); x1t_ready = sem("x1t_ready")
        lt_psum = sem("lt_psum"); lt_ready = sem("lt_ready"); logit_psum = sem("logit_psum"); tanh_ready = sem("tanh_ready")
        step = sem("routing_step"); cmb_ready = sem("cmb_ready")
        cmbt_psum = sem("cmbt_psum"); cmbt_ready = sem("cmbt_ready"); cmb_out = sem("cmb_out")
        wr_in = [sem(f"wr_in{i}") for i in range(2)]; cw_in = [sem(f"cw_in{i}") for i in range(2)]
        gu_hi = sem("gu_hi"); gu_lo = sem("gu_lo"); dn_hi = sem("dn_hi"); dn_lo = sem("dn_lo")
        gu_psum = sem("gu_psum"); tanh_e = sem("tanh_e"); opened = sem("opened"); gated = sem("gated"); weighted = sem("weighted")
        a_hi_ready = sem("a_hi_ready"); a_lo_ready = sem("a_lo_ready"); down_done = sem("down_done")
        zero_ready = sem("zero_ready"); y_ready = sem("y_ready"); y_stored = sem("y_stored")

        block = top.enter_context(nc.Block())
        f = lambda ap: ap.bitcast(F32)

        def wait_alone(eng, semaphore, value, met, met_value):
            value = value if isinstance(value, int) else eng.snap(eng.to_reg(value))
            eng.wait_ge(met, met_value)
            eng.wait_ge(semaphore, value)

        def each_batch(eng, work):
            work(0, 0, 0)
            with eng.Fori(0, NG - 1) as g:
                for i in range(1, 5):
                    work(4 * g + i, i % 4, g + i // 4)
            for B in range(NB - 3, NB):
                work(B, B % 4, B // 4)

        last_batch = lambda B: isinstance(B, int) and B == NB - 1
        batch_cols = lambda B: bass.ds(B * S, S)

        def attention_over(eng):
            eng.wait_ge(cmbt_ready, 2)
            eng.wait_ge(cmb_out, 16)

        @block.sync
        def _(sp):
            sp.dma_start(cst[:], consts).then_inc(const_in, 16)
            def loads(g):
                sp.dma_start(x_g[:], x[:, bass.ds(g * BG, BG), :]).then_inc(x_in, 16)
                sp.dma_start(ctx_f[:], ctx_t[:, :, bass.ds(g * TG, TG)]).then_inc(ctx_in, 16)
            sp.dma_start(wa[:], w_attn).then_inc(weight_in, 16)
            loads(0)
            sp.dma_start(wg[:], w_gate_t).then_inc(weight_in, 16)
            sp.dma_start(cb_qk[:], col_bias).then_inc(bias_in, 16)
            sp.dma_start(rb_vo[:], row_bias.rearrange("(o a) d -> o a d", o=1).to_broadcast([S, 2, D])).then_inc(bias_in, 16)
            sp.dma_start(gb[:], gate_bias.rearrange("(o e) -> o e", o=1).to_broadcast([S, NE])).then_inc(bias_in, 16)
            sp.wait_ge(half_ready, 1)
            sp.dma_start(comb[NE:NX, :], half_rows[:]).then_inc(half_out, 16)

            with sp.Fori(0, NG - 1) as g:
                wait_alone(sp, xn_ready, BG * g + BG, half_ready, 1)
                wait_alone(sp, ctx_lo_ready, g + 1, half_ready, 1)
                sp.wait_ge(ctx_hi_ready, g + 1)
                loads(g + 1)

            def batch_loads(B, j):
                s = j % 2
                for n in range(HC):
                    rows = slice(n * DH, (n + 1) * DH)
                    sp.dma_start(f(k_blocks[rows, s, :, :, n, :]), f(k_all[rows, :, :, batch_cols(B)])).then_inc(kq_in[s], 16)
                sp.dma_start(f(q_now[:, s]), f(q_all[:, :, :, batch_cols(B)])).then_inc(kq_in[s], 16)

            def residual_load(B, j):
                sp.dma_start(x_r[:, j:j + 1, :], x[:, bass.ds(B, 1), :]).then_inc(xr_in[j], 16)

            sp.wait_ge(blocks_zeroed, 2)
            for groups, batches in ((1, (0, 1)), (NG, ())):
                for ready in (k_hi_ready, k_lo_ready, q_hi_ready, q_lo_ready):
                    sp.wait_ge(ready, KC * groups)
                for B in batches:
                    batch_loads(B, B)
                    residual_load(B, B)

            def later_loads(B, j):
                wait_alone(sp, shifted, B - 1, half_ready, 1)
                batch_loads(B, j)
                residual_load(B, j)

            with sp.Fori(0, NG - 1) as g:
                for i in range(2, 6):
                    later_loads(4 * g + i, i % 4)
            for B in range(NB - 2, NB):
                later_loads(B, B % 4)
            def expert_loads(h, e, slot):
                sp.dma_start(w_raw[:, slot, :], w_exp[bass.ds(e, 1), :, :].rearrange("o p n -> p (o n)")).then_inc(wr_in[slot], 16)

            def combine_loads(h, e, slot):
                row = comb[bass.ds(e, 1), h * CPH * TG:(h + 1) * CPH * TG]
                sp.dma_start(cw[:, slot, :], row.to_broadcast([P, CPH * TG])).then_inc(cw_in[slot], 16)

            def free_slot(E):
                wait_alone(sp, gu_lo, E - 1, half_ready, 1)
                sp.wait_ge(dn_lo, E - 1)
                sp.wait_ge(weighted, CPH * (E - 1))

            for slot in range(2):
                expert_loads(0, slot, slot)
            sp.wait_ge(cmbt_ready, 2)
            sp.dma_start(comb[0:NE, :], comb_t[:]).then_inc(cmb_out, 16)
            sp.wait_ge(half_out, 16)
            sp.wait_ge(cmb_out, 16)
            for slot in range(2):
                combine_loads(0, slot, slot)
            def pair_loads(h, e):
                for slot in range(2):
                    free_slot(h * NX + e + slot)
                    expert_loads(h, e + slot, slot)
                    combine_loads(h, e + slot, slot)

            def output_stores(h):
                for c in range(CPH):
                    for m in range(KC):
                        sp.wait_ge(y_ready, (h * CPH + c) * KC + m + 1)
                        sp.dma_start(out_t[m * P:(m + 1) * P, (h * CPH + c) * TG:(h * CPH + c + 1) * TG],
                                     y_out[:, c * KC + m, :]).then_inc(y_stored, 16)

            with sp.Fori(1, NX // 2) as q:
                pair_loads(0, 2 * q)
            pair_loads(1, 0)
            output_stores(0)
            with sp.Fori(1, NX // 2) as q:
                pair_loads(1, 2 * q)
            output_stores(1)
            sp.wait_ge(y_stored, 16 * HALVES * 4)

        @block.gpsimd
        def _(pool):
            pool.memset(half_rows[:], 0.5).then_inc(half_ready, 1)
            pool.memset(pad_f[:, :, :, 0:1], 1.0).then_inc(v_pad, 1)
            pool.memset(pad_f[:, :, :, 1:2], 0.0).then_inc(v_pad, 1)
            pool.wait_ge(v_pad, 2)
            pool.tensor_copy(v_s[:, :, :, DH:VW], pad_f[:]).then_inc(v_pad, 1)
            pool.wait_ge(const_in, 16)
            pool.wait_ge(bias_in, 48)
            with pool.Fori(0, NG) as g:
                pool.wait_ge(ctx_hi_ready, g + 1)
                pool.tensor_tensor(ctx_lo[:], ctx_f[:], f(ctx_hi[:]), ALU.subtract).then_inc(ctx_lo_ready, 1)
                pool.wait_ge(var_ready, g + 1)
                pool.tensor_tensor(rstd[:], ve[:], minus_half, ALU.pow).then_inc(rstd_ready, 1)

            def v_low(B, s):
                pool.wait_ge(v_hi_ready, B + 1)
                pool.tensor_tensor(v_s[:, s, :, VW:VX], v_all[:, bass.ds(B, 1), :].rearrange("p o (h d) -> p (o h) d", d=DH),
                                   f(v_s[:, s, :, 0:DH]), ALU.subtract).then_inc(v_lo_ready, 1)

            def second_rstd(B):
                pool.wait_ge(var2_ready, B + 1)
                pool.tensor_tensor(rstd2[:], ve2[:], minus_half[:, 0:1], ALU.pow).then_inc(rstd2_ready, 1)

            def batch(B, j, turns):
                pool.wait_ge(xr_in[j], 16 * (turns + 1))
                pool.tensor_tensor(x_r[:, j, :], x_r[:, j, :], rb_vo[:, 1, :], ALU.add).then_inc(xr_ready, 1)
                if not (isinstance(B, int) and B == 0):
                    second_rstd(B - 1)
                if not last_batch(B):
                    v_low(B + 1, (j + 1) % 2)

            v_low(0, 0)
            each_batch(pool, batch)
            second_rstd(NB - 1)

            attention_over(pool)
            pool.memset(zero_b[:], 0.0).then_inc(zero_ready, 1)

            def weigh(N, s, E, new_expert):
                if new_expert:
                    pool.wait_ge(cw_in[(s // 2) % 2], 16 * E)
                pool.wait_ge(gated, N + 1)
                pool.tensor_tensor(act[:, s, :], act[:, s, :], cw[:, (s // 2) % 2, (s % 2) * TG:(s % 2 + 1) * TG],
                                   ALU.mult).then_inc(weighted, 1)

            with pool.Fori(0, HALVES * STEPS // 4) as p:
                for s in range(4):
                    weigh(4 * p + s, s, p + 1, s % 2 == 0)

        @block.scalar
        def _(a):
            a.wait_ge(const_in, 16)
            a.activation(ident_r[:], cst[0:S, 0:S], ACT.Copy).then_inc(const_cast, 1)
            a.activation(ident_b[:], cst[0:S, 0:S], ACT.Copy).then_inc(const_cast, 1)
            a.activation(mask_b[:], mask_f[0:S, :], ACT.Copy).then_inc(const_cast, 1)

            def context(g):
                a.wait_ge(ctx_in, 16 * (g + 1))
                a.activation(ctx_hi[:], ctx_f[:], ACT.Copy).then_inc(ctx_hi_ready, 1)

            def projections(g):
                cols = bass.ds(g * TG, TG)
                for m in range(KC):
                    a.wait_ge(k_psum, KC * g + m + 1)
                    a.activation(k_hi_all[:, m, cols], ps[:, m, 0:TG], ACT.Identity,
                                 bias=cb_qk[:, 1, m:m + 1]).then_inc(k_hi_ready, 1)
                a.wait_ge(xt_psum, g + 1)
                a.activation(xt_hi[:], ps[:, 2:2 + KC, 0:TG], ACT.Copy).then_inc(xt_hi_ready, 1)
                if not (isinstance(g, int) and g == NG - 1):
                    a.wait_ge(v_psum, 2 * g + 2)
                    context(g + 1)
                for m in range(KC):
                    a.wait_ge(q_psum, KC * g + m + 1)
                    a.activation(q_hi_all[:, m, cols], ps[:, 6 + m, 0:TG], ACT.Identity,
                                 bias=cb_qk[:, 0, m:m + 1]).then_inc(q_hi_ready, 1)

            context(0)
            a.wait_ge(weight_in, 32)
            a.activation(wa_hi[:], wa[:], ACT.Copy).then_inc(w_hi_ready, 1)
            a.activation(wg_hi[:], wg[:], ACT.Copy).then_inc(w_hi_ready, 1)
            a.wait_ge(bias_in, 48)
            with a.Fori(0, NG - 1) as g:
                projections(g)
            projections(NG - 1)

            def v_high(B, s):
                a.activation(v_s[:, s, :, 0:DH], v_all[:, bass.ds(B, 1), :].rearrange("p o (h d) -> p (o h) d", d=DH),
                             ACT.Copy).then_inc(v_hi_ready, 1)

            def exps(B):
                a.wait_ge(shifted, B + 1)
                for i in range(2):
                    a.activation(prob[:, 2 * i * TG:2 * (i + 1) * TG].rearrange("p (r n) -> p r n", r=2),
                                 ps[0:S, 2 * i:2 * i + 2, 0:TG], ACT.Exp, scale=DH ** -0.5).then_inc(prob_ready, 1)

            def o_high(B):
                a.wait_ge(ot_psum, B + 1)
                a.activation(ot_hi[:], ps[:, 7, 8 * VX:8 * VX + KC * S].rearrange("p (k q) -> p k q", k=KC),
                             ACT.Copy).then_inc(ot_hi_ready, 1)

            def norm_out(B):
                a.wait_ge(ht_psum, B + 1)
                a.activation(h_hi_all[:, :, batch_cols(B)], ps[:, 5, 0:KC * S].rearrange("p (k q) -> p k q", k=KC),
                             ACT.Copy).then_inc(h_hi_ready, 1)
                a.activation(x1t_all[:, :, batch_cols(B)], ps[:, 5, KC * S:2 * KC * S].rearrange("p (k q) -> p k q", k=KC),
                             ACT.Copy).then_inc(x1t_ready, 1)

            def batch(B, j, turns):
                for b in range(QUADS):
                    a.wait_ge(pt_psum, QUADS * B + b + 1)
                    a.activation(pt_hi[:, b % 2, :], ps[0:S, RING[b], 0:TG], ACT.Copy).then_inc(pt_hi_ready, 1)
                    if b == 0 and not (isinstance(B, int) and B == 0):
                        o_high(B - 1)
                if not last_batch(B):
                    v_high(B + 1, (j + 1) % 2)
                    exps(B + 1)
                if not (isinstance(B, int) and B == 0):
                    norm_out(B - 1)

            a.wait_ge(v_ready, 2 * NG)
            v_high(0, 0)
            exps(0)
            each_batch(a, batch)
            o_high(NB - 1)
            norm_out(NB - 1)

            for c in range(NG):
                a.wait_ge(lt_psum, c + 1)
                a.activation(logit_t[:, c * TG:(c + 1) * TG], ps[0:NE, c, 0:TG], ACT.Copy).then_inc(lt_ready, 1)
            a.wait_ge(logit_psum, 1)
            a.activation(rt[:, 0, :], ps[0:S, 4, :], ACT.Tanh, scale=0.5).then_inc(tanh_ready, 1)
            for i in range(2):
                a.wait_ge(cmbt_psum, i + 1)
                a.activation(comb_t[:, 2 * i * TG:2 * (i + 1) * TG].rearrange("p (c t) -> p c t", c=2),
                             ps[0:NE, 2 * i:2 * i + 2, 0:TG], ACT.Copy).then_inc(cmbt_ready, 1)

            def split_gu(loaded, slot):
                a.wait_ge(wr_in[slot], 16 * loaded)
                a.activation(w_hi[:, slot, 0:2 * D], w_raw[:, slot, 0:2 * D], ACT.Copy).then_inc(gu_hi, 1)

            def split_dn(slot):
                a.activation(w_hi[:, slot, 2 * D:], w_raw[:, slot, 2 * D:], ACT.Copy).then_inc(dn_hi, 1)

            def lead(N, s, pair):
                a.wait_ge(gu_psum, N + 1)
                a.activation(act[:, s, :], ps[:, 4 + 2 * (s % 2), 0:TG], ACT.Tanh, scale=0.5).then_inc(tanh_e, 1)

            def split(N, s, pair):
                if s % 2 == 1:
                    split_dn(s // 2)
                elif not (isinstance(N, int) and N // 2 + 1 >= HALVES * NX):
                    split_gu(pair + 1 + s // 2, (s // 2 + 1) % 2)

            def lag(N, s):
                a.wait_ge(weighted, N + 1)
                a.activation(a_hi[:, s, :], act[:, s, :], ACT.Copy).then_inc(a_hi_ready, 1)

            attention_over(a)
            split_gu(1, 0)
            lead(0, 0, 0)
            split(0, 0, 0)
            total = HALVES * STEPS
            with a.Fori(0, total // 4 - 1) as p:
                for s in range(4):
                    k = 4 * p + s
                    lead(k + 1, (s + 1) % 4, p + (s + 1) // 4)
                    lag(k, s)
                    split(k + 1, (s + 1) % 4, p + (s + 1) // 4)
            for k in range(total - 4, total):
                if k + 1 < total:
                    lead(k + 1, (k + 1) % 4, (k + 1) // 4)
                lag(k, k % 4)
                if k + 1 < total:
                    split(k + 1, (k + 1) % 4, (k + 1) // 4)

        @block.vector
        def _(v):
            for s in range(2):
                v.memset(f(k_blocks[:, s]), 0.0).then_inc(blocks_zeroed, 1)
            v.wait_ge(const_in, 16)

            def norm(g):
                wait_alone(v, x_in, 16 * (g + 1), const_in, 16)
                for j in range(BG):
                    v.bn_stats(st[:, j, :], x_g[:, j, :]).then_inc(st_done, 1)
                wait_alone(v, st_done, BG * (g + 1), const_in, 16)
                for j in range(BG):
                    v.bn_aggr(mv[:, j, :], st[:, j, :]).then_inc(mv_done, 1)
                v.wait_ge(mv_done, BG * (g + 1))
                v.tensor_scalar(ve[:], mv[:, :, 1], EPS, None, ALU.add).then_inc(var_ready, 1)
                v.wait_ge(rstd_ready, g + 1)
                for j in range(BG):
                    v.tensor_scalar(xn[:, j, :], x_g[:, j, :], mv[:, j, 0:1], rstd[:, j:j + 1],
                                    ALU.subtract, ALU.mult).then_inc(xn_ready, 1)

            def projections(g):
                cols = bass.ds(g * TG, TG)
                for m in range(KC):
                    v.wait_ge(k_hi_ready, KC * g + m + 1)
                    v.scalar_tensor_tensor(k_lo_all[:, m, cols], ps[:, m, 0:TG], cb_qk[:, 1, m:m + 1],
                                           f(k_hi_all[:, m, cols]), ALU.add, ALU.subtract).then_inc(k_lo_ready, 1)
                v.wait_ge(xt_hi_ready, g + 1)
                v.tensor_tensor(xt_lo[:], ps[:, 2:2 + KC, 0:TG], f(xt_hi[:]), ALU.subtract).then_inc(xt_lo_ready, 1)
                for i in range(2):
                    v.wait_ge(v_psum, 2 * g + i + 1)
                    v.tensor_tensor(v_all[:, bass.ds(g * BG + 2 * i, 2), :],
                                    ps[0:S, 4 + i, :].rearrange("p (b d) -> p b d", b=2),
                                    rb_vo[:, 0, :].unsqueeze(1).to_broadcast([S, 2, D]), ALU.add).then_inc(v_ready, 1)
                if not (isinstance(g, int) and g == NG - 1):
                    norm(g + 1)
                for m in range(KC):
                    v.wait_ge(q_hi_ready, KC * g + m + 1)
                    v.scalar_tensor_tensor(q_lo_all[:, m, cols], ps[:, 6 + m, 0:TG], cb_qk[:, 0, m:m + 1],
                                           f(q_hi_all[:, m, cols]), ALU.add, ALU.subtract).then_inc(q_lo_ready, 1)

            norm(0)
            v.wait_ge(w_hi_ready, 2)
            v.tensor_tensor(wa_lo[:], wa[:], f(wa_hi[:]), ALU.subtract).then_inc(w_lo_ready, 1)
            v.tensor_tensor(wg_lo[:], wg[:], f(wg_hi[:]), ALU.subtract).then_inc(w_lo_ready, 1)
            v.wait_ge(bias_in, 48)
            with v.Fori(0, NG - 1) as g:
                projections(g)
            projections(NG - 1)

            def maximum(B, i):
                v.wait_ge(score_psum, 2 * B + i + 1)
                v.tensor_reduce(nm[:, 8 * i:8 * i + 8].rearrange("p (r n) -> p r n", r=2),
                                ps[0:S, 2 * i:2 * i + 2, 0:TG].rearrange("p r (n k) -> p r n k", k=S), AX.X, ALU.max,
                                negate=True).then_inc(max_ready, 1)

            def split_maximum(B):
                v.wait_ge(max_ready, 2 * B + 2)
                v.tensor_copy(nm_hi[:], nm[:]).then_inc(nm_hi_ready, 1)
                v.wait_ge(nm_hi_ready, B + 1)
                v.tensor_tensor(nm_lo[:], nm[:], f(nm_hi[:]), ALU.subtract).then_inc(nm_ready, 1)

            def low_part(B, b):
                v.wait_ge(pt_hi_ready, QUADS * B + b + 1)
                v.tensor_tensor(pt_lo[:, b % 2, :], ps[0:S, RING[b], 0:TG], f(pt_hi[:, b % 2, :]),
                                ALU.subtract).then_inc(pt_lo_ready, 1)

            def residual(B, j):
                v.wait_ge(xr_ready, B + 1)
                v.wait_ge(proj_psum, B + 1)
                v.tensor_tensor(x1[:, j % 2, :], ps[0:S, 4, 0:D], x_r[:, j, :], ALU.add).then_inc(x1_ready, 1)

            def norm_stats(B, j):
                wait_alone(v, x1_ready, B + 1, const_in, 16)
                v.bn_stats(st2[:], x1[:, j % 2, :]).then_inc(st2_done, 1)
                wait_alone(v, st2_done, B + 1, const_in, 16)
                v.bn_aggr(mv2[:], st2[:]).then_inc(mv2_done, 1)
                v.wait_ge(mv2_done, B + 1)
                v.tensor_scalar(ve2[:], mv2[:, 1:2], EPS, None, ALU.add).then_inc(var2_ready, 1)

            def normalise(B, j):
                v.wait_ge(rstd2_ready, B + 1)
                v.tensor_scalar(h1[:, j % 2, :], x1[:, j % 2, :], mv2[:, 0:1], rstd2[:], ALU.subtract,
                                ALU.mult).then_inc(h1_ready, 1)

            def rows_out(B):
                v.wait_ge(pv_psum, B + 1)
                o = ps[0:S, 6:8, 0:8 * VX].rearrange("p b (h d) -> p b h d", d=VX)
                by_bank = lambda ap: ap.rearrange("p (b h) d -> p b h d", b=2)
                v.tensor_copy(by_bank(o_sum[:]), o[:, :, :, VW:VX]).then_inc(o_read, 1)
                v.reciprocal(rden[:].rearrange("p (b h) -> p b h", b=2), o[:, :, :, DH]).then_inc(o_read, 1)
                v.wait_ge(o_read, 4 * B + 2)
                v.tensor_tensor(by_bank(o_sum[:]), by_bank(o_sum[:]), o[:, :, :, 0:DH], ALU.add).then_inc(o_read, 2)
                v.wait_ge(o_read, 4 * B + 4)
                v.tensor_tensor(on[:].rearrange("p (h d) -> p h d", d=DH), o_sum[:],
                                rden[:].unsqueeze(2).to_broadcast([S, NH, DH]), ALU.mult).then_inc(on_ready, 1)

            def o_low(B):
                v.wait_ge(ot_hi_ready, B + 1)
                v.tensor_tensor(ot_lo[:], ps[:, 7, 8 * VX:8 * VX + KC * S].rearrange("p (k q) -> p k q", k=KC), f(ot_hi[:]),
                                ALU.subtract).then_inc(ot_lo_ready, 1)

            def norm_low(B):
                v.wait_ge(x1t_ready, B + 1)
                v.tensor_tensor(h_lo_all[:, :, batch_cols(B)], ps[:, 5, 0:KC * S].rearrange("p (k q) -> p k q", k=KC),
                                f(h_hi_all[:, :, batch_cols(B)]), ALU.subtract).then_inc(h_lo_ready, 1)

            def batch(B, j, turns):
                first = isinstance(B, int) and B == 0
                more = not last_batch(B)
                low_part(B, 0)
                if more:
                    maximum(B + 1, 0)
                if not first:
                    o_low(B - 1)
                low_part(B, 1)
                if more:
                    maximum(B + 1, 1)
                    split_maximum(B + 1)
                if not first:
                    residual(B - 1, (j - 1) % 4)
                low_part(B, 2)
                if not first:
                    norm_stats(B - 1, (j - 1) % 4)
                low_part(B, 3)
                if not first:
                    normalise(B - 1, (j - 1) % 4)
                rows_out(B)
                if not first:
                    norm_low(B - 1)

            v.sem_inc(h_lo_ready, 1)
            maximum(0, 0)
            maximum(0, 1)
            split_maximum(0)
            each_batch(v, batch)
            o_low(NB - 1)
            residual(NB - 1, (NB - 1) % 4)
            norm_stats(NB - 1, (NB - 1) % 4)
            normalise(NB - 1, (NB - 1) % 4)
            norm_low(NB - 1)

            done = [0]

            def then(*instructions):
                for i in instructions:
                    i.then_inc(step, 1)
                done[0] += len(instructions)
                v.wait_ge(step, done[0])

            def route():
                R = lambda i: rt[:, i, :]
                by_group = lambda ap: ap.rearrange("p (n e) -> p n e", e=EPG)
                v.wait_ge(tanh_ready, 1)
                then(v.tensor_scalar(R(1), R(0), 0.5, 0.5, ALU.mult, ALU.add))
                then(v.tensor_tensor(R(2).rearrange("p (b e) -> p b e", e=NE), R(1).rearrange("p (b e) -> p b e", e=NE),
                                        gb[:].unsqueeze(1).to_broadcast([S, NB, NE]), ALU.add))
                pairs = R(2).rearrange("p (n t) -> p n t", t=2)
                then(v.tensor_tensor(pair_max[:].rearrange("p n t -> p (n t)"), pairs[:, :, 0], pairs[:, :, 1], ALU.max),
                     v.tensor_tensor(pair_min[:].rearrange("p n t -> p (n t)"), pairs[:, :, 0], pairs[:, :, 1], ALU.min))
                then(v.tensor_tensor(gs[:, 0, :], pair_max[:, :, 0], pair_max[:, :, 1], ALU.max),
                     v.tensor_tensor(gs[:, 1, :], pair_max[:, :, 0], pair_max[:, :, 1], ALU.min),
                     v.tensor_tensor(gs[:, 2, :], pair_min[:, :, 0], pair_min[:, :, 1], ALU.max))
                then(v.tensor_tensor(gs[:, 1, :], gs[:, 1, :], gs[:, 2, :], ALU.max))
                then(v.tensor_tensor(gs[:, 0, :], gs[:, 0, :], gs[:, 1, :], ALU.add))
                score = gs[:, 0, :].rearrange("p (b n) -> p b n", n=NGRP)
                own = score.unsqueeze(3).to_broadcast([S, NB, NGRP, NGRP])
                other = score.unsqueeze(2).to_broadcast([S, NB, NGRP, NGRP])
                flat = lambda ap: ap.rearrange("p b n m -> p b (n m)")
                then(v.tensor_tensor(cmpa[:], other, own, ALU.is_gt), v.tensor_tensor(cmpb[:], other, own, ALU.is_equal))
                then(v.tensor_tensor(flat(cmpb[:]), flat(cmpb[:]), earlier.unsqueeze(1).to_broadcast([S, NB, NGRP * NGRP]), ALU.mult))
                then(v.tensor_tensor(cmpa[:], cmpa[:], cmpb[:], ALU.add))
                then(v.tensor_reduce(gs[:, 2, :].rearrange("p (b n) -> p b n", n=NGRP), cmpa[:], AX.X, ALU.add))
                then(v.tensor_scalar(gs[:, 3, :], gs[:, 2, :], float(TOPG), None, ALU.is_lt))
                then(v.tensor_tensor(by_group(R(3)), by_group(R(2)),
                                        gs[:, 3, :].unsqueeze(2).to_broadcast([S, NB * NGRP, EPG]), ALU.mult))
                part_of = lambda i, b: rt[:, i, b * NE:(b + 1) * NE]
                then(*[v.max(best[:, b, :], part_of(3, b)) for b in range(NB)])
                then(*[v.match_replace(part_of(4, b), best[:, b, :], part_of(3, b), TAKEN) for b in range(NB)])
                then(v.tensor_tensor(R(5), R(4), R(3), ALU.not_equal))
                then(v.tensor_tensor(R(6), R(5), R(1), ALU.mult))
                then(v.tensor_reduce(wsum[:, 0, :], R(6).rearrange("p (b e) -> p b e", e=NE), AX.X, ALU.add))
                then(v.tensor_scalar(wsum[:, 1, :], wsum[:, 0, :], 1e-20, None, ALU.add))
                then(v.reciprocal(wsum[:, 0, :], wsum[:, 1, :]))
                v.scalar_tensor_tensor(R(7).rearrange("p (b e) -> p b e", e=NE), R(6).rearrange("p (b e) -> p b e", e=NE),
                                       ROUTE_SCALE / 2, wsum[:, 0, :].unsqueeze(2).to_broadcast([S, NB, NE]),
                                       ALU.mult, ALU.mult).then_inc(cmb_ready, 1)

            route()

            def split_gu(count, slot):
                v.wait_ge(gu_hi, count)
                v.tensor_tensor(w_lo[:, slot, 0:2 * D], w_raw[:, slot, 0:2 * D], f(w_hi[:, slot, 0:2 * D]),
                                ALU.subtract).then_inc(gu_lo, 1)

            def lead(N, s):
                v.wait_ge(tanh_e, N + 1)
                v.scalar_tensor_tensor(act[:, s, :], act[:, s, :], 1.0, ps[:, 4 + 2 * (s % 2), 0:TG], ALU.add,
                                       ALU.mult).then_inc(opened, 1)
                v.wait_ge(opened, N + 1)
                v.tensor_tensor(act[:, s, :], act[:, s, :], ps[:, 5 + 2 * (s % 2), 0:TG], ALU.mult).then_inc(gated, 1)

            def split_at(pair, s, last=False):
                if s % 2 == 1:
                    slot = s // 2
                    v.wait_ge(dn_hi, 2 * pair + slot + 1)
                    v.tensor_tensor(w_lo[:, slot, 2 * D:], w_raw[:, slot, 2 * D:], f(w_hi[:, slot, 2 * D:]),
                                    ALU.subtract).then_inc(dn_lo, 1)
                elif not last:
                    split_gu(2 * pair + s // 2 + 2, (s // 2 + 1) % 2)

            def lag(N, s):
                v.wait_ge(a_hi_ready, N + 1)
                v.tensor_tensor(a_lo[:, s, :], act[:, s, :], f(a_hi[:, s, :]), ALU.subtract).then_inc(a_lo_ready, 1)

            def outputs(h):
                v.wait_ge(down_done, STEPS * (h + 1))
                for c in range(CPH):
                    for m in range(KC):
                        if h:
                            v.wait_ge(y_stored, 16 * (c * KC + m + 1))
                        v.tensor_tensor(y_out[:, c * KC + m, :], ps[:, c * KC + m, 0:TG],
                                        x1t_all[:, m, (h * CPH + c) * TG:(h * CPH + c + 1) * TG],
                                        ALU.add).then_inc(y_ready, 1)

            attention_over(v)
            split_gu(1, 0)
            lead(0, 0)
            split_at(0, 0)
            total = HALVES * STEPS
            for h in range(HALVES):
                with v.Fori(h * STEPS // 4, (h + 1) * STEPS // 4 - (1 if h else 0)) as p:
                    for s in range(4):
                        k = 4 * p + s
                        lead(k + 1, (s + 1) % 4)
                        lag(k, s)
                        split_at(p + (s + 1) // 4, (s + 1) % 4)
                if h == 0:
                    outputs(0)
            for k in range(total - 4, total):
                if k + 1 < total:
                    lead(k + 1, (k + 1) % 4)
                lag(k, k % 4)
                if k + 1 < total:
                    split_at((k + 1) // 4, (k + 1) % 4, last=(k + 1) // 2 + 1 >= HALVES * NX)
            outputs(1)

        @block.tensor
        def _(t):
            def product(out, pairs):
                n = 3 * len(pairs)
                i = 0
                for w_h, w_l, m_h, m_l in pairs:
                    for w, m in ((w_h, m_h), (w_h, m_l), (w_l, m_h)):
                        last = t.matmul(out, w, m, start=(i == 0), stop=(i == n - 1))
                        i += 1
                return last

            t.wait_ge(const_in, 16)
            t.wait_ge(const_cast, 3)
            t.wait_ge(w_lo_ready, 2)
            with t.Fori(0, NG) as g:
                t.wait_ge(ctx_hi_ready, g + 1)
                t.wait_ge(ctx_lo_ready, g + 1)
                for m in range(KC):
                    w = lambda a, k: a[:, 1, k, m * P:(m + 1) * P]
                    product(ps[:, m, 0:TG], [(w(wa_hi, k), w(wa_lo, k), ctx_hi[:, k, :], ctx_lo[:, k, :])
                                             for k in range(KC)]).then_inc(k_psum, 1)
                t.wait_ge(xn_ready, BG * (g + 1))
                for k in range(KC):
                    for j in range(BG):
                        last = t.transpose(ps[:, 2 + k, j * S:(j + 1) * S], xn[:, j, k * P:(k + 1) * P], ident[0:S, 0:S])
                last.then_inc(xt_psum, 1)
                for j in range(BG):
                    c = lambda a, k: a[:, k, j * S:(j + 1) * S]
                    last = product(ps[0:S, 4 + j // 2, (j % 2) * D:(j % 2 + 1) * D],
                                   [(c(ctx_hi, k), c(ctx_lo, k), wa_hi[:, 2, k, :], wa_lo[:, 2, k, :]) for k in range(KC)])
                    if j % 2:
                        last.then_inc(v_psum, 1)
                t.wait_ge(xt_hi_ready, g + 1)
                t.wait_ge(xt_lo_ready, g + 1)
                for m in range(KC):
                    w = lambda a, k: a[:, 0, k, m * P:(m + 1) * P]
                    product(ps[:, 6 + m, 0:TG], [(w(wa_hi, k), w(wa_lo, k), xt_hi[:, k, :], xt_lo[:, k, :])
                                                 for k in range(KC)]).then_inc(q_psum, 1)
                t.wait_ge(k_lo_ready, KC * (g + 1))
                t.wait_ge(v_ready, 2 * (g + 1))

            def scores(B, j, b):
                s = j % 2
                m, n = b // 2, slice(4 * (b % 2), 4 * (b % 2) + 4)
                out = ps[0:S, b, 0:TG]
                t.matmul(out, ident_b[:], mask_b[:], start=True, stop=False, skip_group_check=True)
                for q_part, k_part in ((0, 0), (0, 1), (1, 0)):
                    last = t.matmul(out, q_now[:, s, q_part, m, :], k_blocks[:, s, k_part, m, n, :], start=False, stop=False,
                                    skip_group_check=True)
                return last

            def half_scores(B, j, turns, i):
                if i == 0:
                    t.wait_ge(kq_in[j % 2], KQ_DMAS * 16 * (2 * turns + j // 2 + 1))
                for b in (2 * i, 2 * i + 1):
                    last = scores(B, j, b)
                last.then_inc(score_psum, 1)

            def shift(B):
                t.wait_ge(nm_ready, B + 1)
                for b in range(QUADS):
                    for part_of in (nm_hi, nm_lo):
                        last = t.matmul(ps[0:S, b, 0:TG], ident_r[:],
                                        part_of[:, 4 * b:4 * b + 4].unsqueeze(2).to_broadcast([S, 4, S]),
                                        start=False, stop=part_of is nm_lo, skip_group_check=True)
                last.then_inc(shifted, 1)

            def turn(B, b):
                for n in range(4):
                    last = t.transpose(ps[0:S, RING[b], n * S:(n + 1) * S],
                                       prob[:, (4 * b + n) * S:(4 * b + n + 1) * S], ident[0:S, 0:S])
                last.then_inc(pt_psum, 1)

            def values(B, j, b):
                if b == 0:
                    t.wait_ge(v_lo_ready, B + 1)
                t.wait_ge(pt_hi_ready, QUADS * B + b + 1)
                t.wait_ge(pt_lo_ready, QUADS * B + b + 1)
                for n in range(4):
                    h = 4 * b + n
                    c = slice(n * S, (n + 1) * S)
                    at = (h % 8) * VX
                    t.matmul(ps[0:S, 6 + h // 8, at:at + VX], pt_hi[:, b % 2, c], v_s[:, j % 2, h, :], start=True, stop=False,
                             skip_group_check=True)
                    last = t.matmul(ps[0:S, 6 + h // 8, at:at + VW], pt_lo[:, b % 2, c], v_s[:, j % 2, h, 0:VW], start=False,
                                    stop=True, skip_group_check=True)
                return last

            def turn_output(B):
                t.wait_ge(on_ready, B + 1)
                for k in range(KC):
                    last = t.transpose(ps[:, 7, 8 * VX + k * S:8 * VX + (k + 1) * S], on[:, k * P:(k + 1) * P], ident[0:S, 0:S])
                last.then_inc(ot_psum, 1)

            def project(B):
                t.wait_ge(ot_hi_ready, B + 1)
                t.wait_ge(ot_lo_ready, B + 1)
                product(ps[0:S, 4, 0:D], [(ot_hi[:, k, :], ot_lo[:, k, :], wa_hi[:, 3, k, :], wa_lo[:, 3, k, :])
                                          for k in range(KC)]).then_inc(proj_psum, 1)

            def turn_rows(B, j):
                t.wait_ge(h1_ready, B + 1)
                for i, rows in enumerate((h1, x1)):
                    for k in range(KC):
                        last = t.transpose(ps[:, 5, (KC * i + k) * S:(KC * i + k + 1) * S],
                                           rows[:, j % 2, k * P:(k + 1) * P], ident[0:S, 0:S])
                last.then_inc(ht_psum, 1)

            def batch(B, j, turns):
                first = isinstance(B, int) and B == 0
                more = not last_batch(B)
                ahead = (B + 1, (j + 1) % 4, turns + (j + 1) // 4)
                t.wait_ge(prob_ready, 2 * B + 1)
                turn(B, 0)
                if more:
                    half_scores(*ahead, 0)
                if not first:
                    turn_output(B - 1)
                    t.wait_ge(h_lo_ready, B)
                turn(B, 1)
                t.wait_ge(prob_ready, 2 * B + 2)
                if more:
                    half_scores(*ahead, 1)
                values(B, j, 0)
                if not first:
                    project(B - 1)
                values(B, j, 1)
                turn(B, 2)
                if not first:
                    t.wait_ge(x1_ready, B)
                turn(B, 3)
                if more:
                    shift(B + 1)
                values(B, j, 2)
                values(B, j, 3).then_inc(pv_psum, 1)
                if not first:
                    turn_rows(B - 1, (j - 1) % 4)

            t.wait_ge(v_pad, 3)
            half_scores(0, 0, 0, 0)
            half_scores(0, 0, 0, 1)
            shift(0)
            each_batch(t, batch)

            def logits(c):
                t.wait_ge(h_lo_ready, BG * (c + 1) + 1)
                cols = slice(c * TG, (c + 1) * TG)
                product(ps[0:NE, c, 0:TG], [(wg_hi[:, k, :], wg_lo[:, k, :], h_hi_all[:, k, cols], h_lo_all[:, k, cols])
                                            for k in range(KC)]).then_inc(lt_psum, 1)

            logits(0)
            turn_output(NB - 1)
            logits(1)
            project(NB - 1)
            logits(2)
            t.wait_ge(h_lo_ready, NB)
            turn_rows(NB - 1, (NB - 1) % 4)
            for b in range(NB):
                if b == NB - BG:
                    logits(NG - 1)
                t.wait_ge(lt_ready, b // BG + 1)
                last = t.transpose(ps[0:S, 4, b * NE:(b + 1) * NE], logit_t[:, b * S:(b + 1) * S], ident[0:NE, 0:NE])
            last.then_inc(logit_psum, 1)
            t.wait_ge(cmb_ready, 1)
            for b in range(NB):
                last = t.transpose(ps[0:NE, b // BG, (b % BG) * S:(b % BG + 1) * S], rt[:, 7, b * NE:(b + 1) * NE],
                                   ident[0:S, 0:S])
                if b % 8 == 7:
                    last.then_inc(cmbt_psum, 1)

            def gate_up(N, s, col, experts):
                slot = s // 2
                if s % 2 == 0:
                    t.wait_ge(gu_hi, experts)
                    t.wait_ge(gu_lo, experts)
                if not (isinstance(N, int) and N < 2):
                    t.wait_ge(gated, N - 1)
                for part_of in range(2):
                    w = lambda a, k: a[:, slot, (2 * part_of + k) * P:(2 * part_of + k + 1) * P]
                    last = product(ps[:, 4 + 2 * (s % 2) + part_of, 0:TG],
                                   [(w(w_hi, k), w(w_lo, k), h_hi_all[:, k, col:col + TG], h_lo_all[:, k, col:col + TG])
                                    for k in range(KC)])
                last.then_inc(gu_psum, 1)

            def down(k, s, experts):
                slot = s // 2
                if s % 2 == 0:
                    t.wait_ge(dn_hi, experts)
                    t.wait_ge(dn_lo, experts)
                t.wait_ge(a_hi_ready, k + 1)
                t.wait_ge(a_lo_ready, k + 1)
                for m in range(KC):
                    w = lambda a: a[:, slot, 2 * D + m * P:2 * D + (m + 1) * P]
                    for i, (ww, mm) in enumerate(((w_hi, a_hi), (w_hi, a_lo), (w_lo, a_hi))):
                        last = t.matmul(ps[:, (s % 2) * KC + m, 0:TG], w(ww), mm[:, s, :], start=False, stop=False,
                                        skip_group_check=True)
                last.then_inc(down_done, 1)

            gate_up(0, 0, 0, 1)
            gate_up(1, 1, TG, 1)
            total = HALVES * STEPS
            for h in range(HALVES):
                t.wait_ge(zero_ready, 1)
                if h:
                    t.wait_ge(y_ready, 4)
                for b in range(CPH * KC):
                    t.matmul(ps[:, b, 0:TG], zero_b[:, 0:P], zero_b[:], start=True, stop=False, skip_group_check=True)
                col = lambda c, later: ((h + later) * CPH + c) * TG

                with t.Fori(h * STEPS // 4, (h + 1) * STEPS // 4 - 1) as p:
                    for s in range(4):
                        gate_up(4 * p + s + 2, (s + 2) % 4, col(s % 2, 0), 2 * p + s // 2 + 2)
                        down(4 * p + s, s, 2 * p + s // 2 + 1)
                for s in range(4):
                    N = (h + 1) * STEPS - 4 + s
                    if N + 2 < total:
                        gate_up(N + 2, (s + 2) % 4, col(s % 2, 1 if s >= 2 else 0), N // 2 + 2)
                    down(N, s, N // 2 + 1)


def constants():
    import numpy as np
    cst = np.zeros((P, CST), np.float32)
    cst[:, 0:P] = np.eye(P)
    causal = np.where(np.arange(S)[None, :] <= np.arange(S)[:, None], 0.0, MASKED)
    cst[0:S, P:P + TG] = np.tile(causal, (1, 4))
    g = np.arange(NGRP)
    cst[:, P + TG:P + TG + NGRP * NGRP] = (g[None, :] < g[:, None]).reshape(1, -1)
    cst[:, -BG:] = -0.5
    return cst


def kernel(x, ctx_1024, L0_xattn_Wq, L0_xattn_bq, L0_xattn_Wk, L0_xattn_bk, L0_xattn_Wv, L0_xattn_bv, L0_xattn_Wo,
           L0_xattn_bo, L0_ffn_gate_w, L0_ffn_gate_bias, L0_ffn_w_gate, L0_ffn_w_up, L0_ffn_w_down, L0_ffn_sh_gate,
           L0_ffn_sh_up, L0_ffn_sh_down):
    import numpy as np
    import concourse.bacc as bacc
    from concourse.bass_utils import run_bass_kernel_spmd

    A = np.asarray
    rows = lambda w: A(w).reshape(KC, P, -1).transpose(1, 0, 2)
    turned = lambda w: A(w).transpose(0, 2, 1)
    gate = np.concatenate([turned(L0_ffn_w_gate), turned(A(L0_ffn_sh_gate).reshape(2, FI, D))])
    up = np.concatenate([turned(L0_ffn_w_up), turned(A(L0_ffn_sh_up).reshape(2, FI, D))])
    down = np.concatenate([turned(L0_ffn_w_down), A(L0_ffn_sh_down).T.reshape(2, FI, D)])
    by_chunk = lambda w: w.reshape(NX, KC, P, FI).transpose(0, 2, 1, 3).reshape(NX, P, KC * FI)
    arrays = {
        "x": A(x).transpose(1, 0, 2),
        "ctx_t": A(ctx_1024)[:, :S].transpose(2, 0, 1).reshape(KC, P, T).transpose(1, 0, 2),
        "w_attn": np.stack([rows(w) for w in (L0_xattn_Wq, L0_xattn_Wk, L0_xattn_Wv, L0_xattn_Wo)], 1),
        "w_gate_t": rows(A(L0_ffn_gate_w).T),
        "col_bias": np.stack([A(b).reshape(KC, P).T for b in (L0_xattn_bq, L0_xattn_bk)], 1),
        "row_bias": np.stack([A(L0_xattn_bv), A(L0_xattn_bo)]),
        "gate_bias": A(L0_ffn_gate_bias),
        "w_exp": np.concatenate([by_chunk(gate), by_chunk(up), down], 2),
        "consts": constants(),
    }
    arrays = {k: np.ascontiguousarray(a) for k, a in arrays.items()}
    nc = bacc.Bacc("TRN2", target_bir_lowering=False, num_devices=1)
    args = [nc.dram_tensor(k, a.shape, mybir.dt.from_np(a.dtype), kind="ExternalInput").ap() for k, a in arrays.items()]
    out_t = nc.dram_tensor("out_t", (D, T), F32, kind="ExternalOutput").ap()
    block_kernel(nc, *args, out_t)
    r = run_bass_kernel_spmd(nc, [arrays], core_ids=[0])
    return np.ascontiguousarray(r.results[0]["out_t"].T).reshape(NB, S, D)
```

```python
from contextlib import ExitStack

import concourse.bass as bass
from concourse import mybir

ALU = mybir.AluOpType
ACT = mybir.ActivationFunctionType
AX = mybir.AxisListType
F32 = mybir.dt.float32
F32R = mybir.dt.float32r
BF16 = mybir.dt.bfloat16

P = 128
D = 256
KC = D // P
NB = 16
S = 100
NG = 4
BG = NB // NG
TG = BG * S
T = NB * S
NH = 16
DH = D // NH
HC = NH // KC
QUADS = NH // 4
VW = DH + 2
VX = VW + DH
KQ_DMAS = HC + 1
NE = 32
NX = NE + 2
FI = 128
NGRP = 8
EPG = NE // NGRP
TOPG = 4
EPS = 1e-5
ROUTE_SCALE = 2.5
HALVES = 2
CPH = 2
STEPS = NX * CPH
CST = P + TG + BG
MASKED = -1e30
TAKEN = -3e38
NOWHERE = -2e38
WEIGHT_ORDER = (1, 2, 0, 3)
RING = (4, 5, 5, 4)



def block_kernel(nc, x, ctx_t, w_attn, w_gate_t, col_bias, row_bias, gate_bias, w_exp, consts, out_t):
    comb = nc.dram_tensor("combine_rows", (NX, T), F32).ap()

    with ExitStack() as top:
        sem = lambda name: top.enter_context(nc.semaphore(name))
        keep = lambda name, shape, dt=F32: top.enter_context(nc.sbuf_tensor(name, shape, dt))
        ps = top.enter_context(nc.psum_tensor("ps", [P, 8, 512], F32))

        proj_part = ExitStack()
        tmp = lambda name, shape, dt=F32: proj_part.enter_context(nc.sbuf_tensor(name, shape, dt))
        x_g = tmp("x_g", [S, BG, D])
        ctx_f = tmp("ctx_f", [P, KC, TG])
        ctx_hi = tmp("ctx_hi", [P, KC, TG], F32R)
        ctx_lo = tmp("ctx_lo", [P, KC, TG], F32R)
        xn = tmp("xn", [S, BG, D])
        xt_hi = tmp("xt_hi", [P, KC, TG], F32R)
        xt_lo = tmp("xt_lo", [P, KC, TG], F32R)
        st = tmp("st", [S, BG, 6])
        mv = tmp("mv", [S, BG, 2])
        ve = tmp("ve", [S, BG])
        rstd = tmp("rstd", [S, BG])
        proj_part.close()

        x1t_all = keep("x1t_all", [P, KC, T])
        h_hi_all = keep("h_hi_all", [P, KC, T], F32R)
        h_lo_all = keep("h_lo_all", [P, KC, T], F32R)
        w_raw = keep("w_raw", [P, 2, 3 * D])

        cst = keep("cst", [P, CST])
        gb = keep("gb", [S, NE])

        part = ExitStack()
        tmp = lambda name, shape, dt=F32: part.enter_context(nc.sbuf_tensor(name, shape, dt))
        ident = cst[:, 0:128]
        mask_f = cst[:, 128:128 + TG]
        minus_half = cst[0:S, 528:532]
        ident_b = tmp("ident_b", [S, S], BF16)
        mask_b = tmp("mask_b", [S, TG], BF16)
        wa = tmp("wa", [P, 4, KC, D])
        wa_hi = tmp("wa_hi", [P, 4, KC, D], F32R)
        wa_lo = tmp("wa_lo", [P, 4, KC, D], F32R)
        wg = tmp("wg", [P, KC, NE])
        wg_hi = tmp("wg_hi", [P, KC, NE], F32R)
        wg_lo = tmp("wg_lo", [P, KC, NE], F32R)
        cb_qk = tmp("cb_qk", [P, 2, KC])
        rb_vo = tmp("rb_vo", [S, 2, D])
        half_rows = tmp("half_rows", [2 * NG, TG])
        q_all = tmp("q_all", [P, 2, KC, T], F32R)
        k_all = tmp("k_all", [P, 2, KC, T], F32R)
        q_hi_all, q_lo_all = q_all[:, 0], q_all[:, 1]
        k_hi_all, k_lo_all = k_all[:, 0], k_all[:, 1]
        v_all = tmp("v_all", [S, NB, D])
        pass_part = ExitStack()
        loop = lambda name, shape, dt=F32: pass_part.enter_context(nc.sbuf_tensor(name, shape, dt))
        k_blocks = loop("k_blocks", [P, 2, 2, KC, HC, S], F32R)
        q_now = loop("q_now", [P, 2, 2, KC, S], F32R)
        v_s = loop("v_s", [S, 2, NH, VX], F32R)
        pad_f = loop("pad_f", [S, 2, NH, 2])
        nm = loop("nm", [S, NH])
        nm_scaled = loop("nm_scaled", [S, NH])
        prob = loop("prob", [S, 2, NH * S])
        pt_hi = loop("pt_hi", [S, 2, 4 * S], F32R)
        pt_lo = loop("pt_lo", [S, 2, 4 * S], F32R)
        rden = loop("rden", [S, NH])
        o_sum = loop("o_sum", [S, NH, DH])
        on = loop("on", [S, D])
        ot_hi = loop("ot_hi", [P, KC, S], F32R)
        ot_lo = loop("ot_lo", [P, KC, S], F32R)
        x_r = loop("x_r", [S, 4, D])
        x1 = loop("x1", [S, 2, D])
        h1 = loop("h1", [S, 2, D])
        st2 = loop("st2", [S, 6])
        mv2 = loop("mv2", [S, 2])
        ve2 = loop("ve2", [S, 1])
        rstd2 = loop("rstd2", [S, 1])
        pass_part.close()
        logit_t = tmp("logit_t", [NE, T])
        rt = tmp("rt", [S, 8, NB * NE])
        pair_max = tmp("pair_max", [S, NB * NGRP, 2])
        pair_min = tmp("pair_min", [S, NB * NGRP, 2])
        gs = tmp("gs", [S, 4, NB * NGRP])
        best = tmp("best", [S, NB, 8])
        wsum = tmp("wsum", [S, 2, NB])
        comb_t = tmp("comb_t", [NE, T])
        part.close()

        w_hi = keep("w_hi", [P, 2, 3 * D], F32R)
        w_lo = keep("w_lo", [P, 2, 3 * D], F32R)
        cw = keep("cw", [P, 2, CPH * TG])
        act = keep("act", [P, 4, TG])
        a_hi = keep("a_hi", [P, 4, TG], F32R)
        a_lo = keep("a_lo", [P, 4, TG], F32R)
        y_out = keep("y_out", [P, 4, TG])
        zero_b = keep("zero_b", [P, TG], BF16)

        const_in = sem("const_in"); weight_in = [sem(f"weight_in{i}") for i in range(4)]; gate_in = sem("gate_in"); bias_in = sem("bias_in")
        const_cast = sem("const_cast"); w_hi_ready = sem("w_hi_ready"); w_lo_ready = sem("w_lo_ready")
        v_pad = sem("v_pad"); blocks_zeroed = sem("blocks_zeroed"); half_ready = sem("half_ready"); half_out = sem("half_out")
        x_in = sem("x_in"); ctx_in = sem("ctx_in")
        st_done = sem("st_done"); mv_done = sem("mv_done"); var_ready = sem("var_ready")
        rstd_ready = sem("rstd_ready"); xn_ready = sem("xn_ready")
        ctx_hi_ready = sem("ctx_hi_ready"); ctx_lo_ready = sem("ctx_lo_ready")
        k_psum = sem("k_psum"); k_hi_ready = sem("k_hi_ready"); k_lo_ready = sem("k_lo_ready")
        xt_psum = sem("xt_psum"); xt_hi_ready = sem("xt_hi_ready"); xt_lo_ready = sem("xt_lo_ready")
        v_psum = sem("v_psum"); v_ready = sem("v_ready")
        q_psum = sem("q_psum"); q_hi_ready = sem("q_hi_ready"); q_lo_ready = sem("q_lo_ready")
        kq_in = [sem(f"kq_in{i}") for i in range(2)]; xr_in = [sem(f"xr_in{i}") for i in range(4)]
        xr_ready = sem("xr_ready"); v_hi_ready = sem("v_hi_ready"); v_lo_ready = sem("v_lo_ready")
        score_psum = sem("score_psum"); max_ready = sem("max_ready"); nm_ready = sem("nm_ready")
        prob_ready = sem("prob_ready")
        pt_psum = sem("pt_psum"); pt_hi_ready = sem("pt_hi_ready"); pt_lo_ready = sem("pt_lo_ready")
        pv_psum = sem("pv_psum"); o_read = sem("o_read"); on_ready = sem("on_ready")
        ot_psum = sem("ot_psum"); ot_hi_ready = sem("ot_hi_ready"); ot_lo_ready = sem("ot_lo_ready")
        proj_psum = sem("proj_psum"); x1_ready = sem("x1_ready")
        st2_done = sem("st2_done"); mv2_done = sem("mv2_done"); var2_ready = sem("var2_ready")
        rstd2_ready = sem("rstd2_ready"); h1_ready = sem("h1_ready")
        ht_psum = sem("ht_psum"); h_hi_ready = sem("h_hi_ready"); h_lo_ready = sem("h_lo_ready"); x1t_ready = sem("x1t_ready")
        lt_psum = sem("lt_psum"); lt_ready = sem("lt_ready"); logit_psum = sem("logit_psum"); tanh_ready = sem("tanh_ready")
        step = sem("routing_step"); cmb_ready = sem("cmb_ready")
        cmbt_psum = sem("cmbt_psum"); cmbt_ready = sem("cmbt_ready"); cmb_out = sem("cmb_out")
        wr_in = [sem(f"wr_in{i}") for i in range(2)]; wd_in = [sem(f"wd_in{i}") for i in range(2)]; cw_in = [sem(f"cw_in{i}") for i in range(2)]
        gu_hi = sem("gu_hi"); gu_lo = sem("gu_lo"); dn_hi = sem("dn_hi"); dn_lo = sem("dn_lo")
        gu_psum = sem("gu_psum"); tanh_e = sem("tanh_e"); opened = sem("opened"); gated = sem("gated"); weighted = sem("weighted")
        a_hi_ready = sem("a_hi_ready"); a_lo_ready = sem("a_lo_ready"); down_done = sem("down_done")
        zero_ready = sem("zero_ready"); y_ready = sem("y_ready"); y_stored = sem("y_stored")

        block = top.enter_context(nc.Block())
        f = lambda ap: ap.bitcast(F32)

        def wait_alone(eng, semaphore, value, met, met_value):
            value = value if isinstance(value, int) else eng.snap(eng.to_reg(value))
            eng.wait_ge(met, met_value)
            eng.wait_ge(semaphore, value)

        def each_batch(eng, work):
            work(0, 0, 0)
            with eng.Fori(0, NG - 1) as g:
                for i in range(1, 5):
                    work(4 * g + i, i % 4, g + i // 4)
            for B in range(NB - 3, NB):
                work(B, B % 4, B // 4)

        last_batch = lambda B: isinstance(B, int) and B == NB - 1
        batch_cols = lambda B: bass.ds(B * S, S)

        def attention_over(eng):
            eng.wait_ge(tanh_ready, 1)
            eng.wait_ge(half_out, 16)

        @block.sync
        def _(sp):
            def rows_load(g):
                sp.dma_start(x_g[:], x[:, bass.ds(g * BG, BG), :]).then_inc(x_in, 16)

            def context_load(g):
                sp.dma_start(ctx_f[:], ctx_t[:, :, bass.ds(g * TG, TG)]).then_inc(ctx_in, 16)

            rows_load(0)
            context_load(0)
            sp.dma_start(cst[:], consts).then_inc(const_in, 16)
            for i in WEIGHT_ORDER:
                sp.dma_start(wa[:, i, :, :], w_attn[:, i, :, :]).then_inc(weight_in[i], 16)
            sp.dma_start(wg[:], w_gate_t).then_inc(gate_in, 16)
            sp.dma_start(cb_qk[:], col_bias).then_inc(bias_in, 16)
            sp.dma_start(rb_vo[:], row_bias.rearrange("(o a) d -> o a d", o=1).to_broadcast([S, 2, D])).then_inc(bias_in, 16)
            sp.dma_start(gb[:], gate_bias.rearrange("(o e) -> o e", o=1).to_broadcast([S, NE])).then_inc(bias_in, 16)
            sp.wait_ge(half_ready, 1)
            sp.dma_start(comb[0:NX - NE, :].rearrange("e (c t) -> (e c) t", t=TG), half_rows[:]).then_inc(half_out, 16)

            with sp.Fori(0, NG - 1) as g:
                wait_alone(sp, xn_ready, BG * g + BG, half_ready, 1)
                rows_load(g + 1)
                wait_alone(sp, ctx_lo_ready, g + 1, half_ready, 1)
                context_load(g + 1)

            def batch_loads(B, j):
                s = j % 2
                for n in range(HC):
                    rows = slice(n * DH, (n + 1) * DH)
                    sp.dma_start(f(k_blocks[rows, s, :, :, n, :]), f(k_all[rows, :, :, batch_cols(B)])).then_inc(kq_in[s], 16)
                sp.dma_start(f(q_now[:, s]), f(q_all[:, :, :, batch_cols(B)])).then_inc(kq_in[s], 16)

            def residual_load(B, j):
                sp.dma_start(x_r[:, j:j + 1, :], x[:, bass.ds(B, 1), :]).then_inc(xr_in[j], 16)

            sp.wait_ge(blocks_zeroed, 2)
            for groups, batches in ((1, (0, 1)), (NG, ())):
                sp.wait_ge(k_lo_ready, KC * (groups + 1))
                sp.wait_ge(q_lo_ready, KC * groups)
                for B in batches:
                    batch_loads(B, B)
            residual_load(0, 0)

            def later_loads(B, j):
                wait_alone(sp, score_psum, 2 * (B - 1), half_ready, 1)
                batch_loads(B, j)
                residual_load(B - 1, (j - 1) % 4)

            with sp.Fori(0, NG - 1) as g:
                for i in range(2, 6):
                    later_loads(4 * g + i, i % 4)
            for B in range(NB - 2, NB):
                later_loads(B, B % 4)
            sp.wait_ge(x1_ready, NB - 4)
            residual_load(NB - 1, (NB - 1) % 4)
            def gate_up_load(e, slot):
                sp.dma_start(w_raw[:, slot, 0:2 * D],
                             w_exp[bass.ds(e, 1), :, 0:2 * D].rearrange("o p n -> p (o n)")).then_inc(wr_in[slot], 16)

            def down_load(e, slot):
                sp.dma_start(w_raw[:, slot, 2 * D:],
                             w_exp[bass.ds(e, 1), :, 2 * D:].rearrange("o p n -> p (o n)")).then_inc(wd_in[slot], 16)

            def combine_loads(h, e, slot):
                row = comb[bass.ds(e, 1), h * CPH * TG:(h + 1) * CPH * TG]
                sp.dma_start(cw[:, slot, :], row.to_broadcast([P, CPH * TG])).then_inc(cw_in[slot], 16)

            for slot in range(2):
                gate_up_load(slot, slot)
                down_load(slot, slot)
            attention_over(sp)
            for slot in range(2):
                combine_loads(0, slot, slot)
            sp.wait_ge(cmbt_ready, 2)
            sp.dma_start(comb[NX - NE:NX, :], comb_t[:]).then_inc(cmb_out, 16)
            sp.wait_ge(cmb_out, 16)
            def pair_loads(h, e):
                for slot in range(2):
                    E = h * NX + e + slot
                    wait_alone(sp, gu_lo, E - 1, half_ready, 1)
                    gate_up_load(e + slot, slot)
                    wait_alone(sp, dn_lo, E - 1, half_ready, 1)
                    down_load(e + slot, slot)
                    wait_alone(sp, weighted, CPH * (E - 1), half_ready, 1)
                    combine_loads(h, e + slot, slot)

            def output_stores(h):
                for c in range(CPH):
                    for m in range(KC):
                        sp.wait_ge(y_ready, (h * CPH + c) * KC + m + 1)
                        sp.dma_start(out_t[m * P:(m + 1) * P, (h * CPH + c) * TG:(h * CPH + c + 1) * TG],
                                     y_out[:, c * KC + m, :]).then_inc(y_stored, 16)

            with sp.Fori(1, NX // 2) as q:
                pair_loads(0, 2 * q)
            pair_loads(1, 0)
            output_stores(0)
            with sp.Fori(1, NX // 2) as q:
                pair_loads(1, 2 * q)
            output_stores(1)
            sp.wait_ge(y_stored, 16 * HALVES * 4)

        @block.gpsimd
        def _(pool):
            for s in range(2):
                pool.memset(f(k_blocks[:, s]), 0.0).then_inc(blocks_zeroed, 1)
            pool.memset(half_rows[:], 0.5).then_inc(half_ready, 1)
            pool.memset(pad_f[:, :, :, 0:1], 1.0).then_inc(v_pad, 1)
            pool.memset(pad_f[:, :, :, 1:2], 0.0).then_inc(v_pad, 1)
            pool.wait_ge(v_pad, 2)
            pool.tensor_copy(v_s[:, :, :, DH:VW], pad_f[:]).then_inc(v_pad, 1)
            pool.wait_ge(const_in, 16)
            with pool.Fori(0, NG) as g:
                pool.wait_ge(var_ready, g + 1)
                pool.tensor_tensor(rstd[:], ve[:], minus_half, ALU.pow).then_inc(rstd_ready, 1)
                pool.wait_ge(ctx_hi_ready, g + 1)
                pool.tensor_tensor(ctx_lo[:], ctx_f[:], f(ctx_hi[:]), ALU.subtract).then_inc(ctx_lo_ready, 1)

            def v_low(B, s):
                pool.wait_ge(v_hi_ready, B + 1)
                pool.tensor_tensor(v_s[:, s, :, VW:VX], v_all[:, bass.ds(B, 1), :].rearrange("p o (h d) -> p (o h) d", d=DH),
                                   f(v_s[:, s, :, 0:DH]), ALU.subtract).then_inc(v_lo_ready, 1)

            def second_rstd(B):
                pool.wait_ge(var2_ready, B + 1)
                pool.tensor_tensor(rstd2[:], ve2[:], minus_half[:, 0:1], ALU.pow).then_inc(rstd2_ready, 1)

            def batch(B, j, turns):
                pool.wait_ge(xr_in[j], 16 * (turns + 1))
                pool.tensor_tensor(x_r[:, j, :], x_r[:, j, :], rb_vo[:, 1, :], ALU.add).then_inc(xr_ready, 1)
                if not (isinstance(B, int) and B == 0):
                    second_rstd(B - 1)
                if not last_batch(B):
                    v_low(B + 1, (j + 1) % 2)

            pool.wait_ge(bias_in, 48)
            v_low(0, 0)
            each_batch(pool, batch)
            second_rstd(NB - 1)

            attention_over(pool)
            pool.memset(zero_b[:], 0.0).then_inc(zero_ready, 1)

            def weigh(N, s, E, new_expert):
                if new_expert:
                    pool.wait_ge(cw_in[(s // 2) % 2], 16 * E)
                pool.wait_ge(gated, N + 1)
                pool.tensor_tensor(act[:, s, :], act[:, s, :], cw[:, (s // 2) % 2, (s % 2) * TG:(s % 2 + 1) * TG],
                                   ALU.mult).then_inc(weighted, 1)

            with pool.Fori(0, HALVES * STEPS // 4) as p:
                for s in range(4):
                    weigh(4 * p + s, s, p + 1, s % 2 == 0)

        @block.scalar
        def _(a):
            def context(g):
                a.wait_ge(ctx_in, 16 * (g + 1))
                a.activation(ctx_hi[:], ctx_f[:], ACT.Copy).then_inc(ctx_hi_ready, 1)

            def projections(g):
                cols = bass.ds(g * TG, TG)
                a.wait_ge(xt_psum, g + 1)
                a.activation(xt_hi[:], ps[:, 2:2 + KC, 0:TG], ACT.Copy).then_inc(xt_hi_ready, 1)
                for m in range(KC):
                    a.wait_ge(k_psum, KC * g + m + 1)
                    a.activation(k_hi_all[:, m, cols], ps[:, m, 0:TG], ACT.Identity,
                                 bias=cb_qk[:, 1, m:m + 1]).then_inc(k_hi_ready, 1)
                if not (isinstance(g, int) and g == NG - 1):
                    a.wait_ge(v_psum, 2 * g + 2)
                    context(g + 1)
                for m in range(KC):
                    a.wait_ge(q_psum, KC * g + m + 1)
                    a.activation(q_hi_all[:, m, cols], ps[:, 6 + m, 0:TG], ACT.Identity,
                                 bias=cb_qk[:, 0, m:m + 1]).then_inc(q_hi_ready, 1)

            context(0)
            for i in WEIGHT_ORDER:
                a.wait_ge(weight_in[i], 16)
                a.activation(wa_hi[:, i, :, :], wa[:, i, :, :], ACT.Copy).then_inc(w_hi_ready, 1)
            a.wait_ge(gate_in, 16)
            a.activation(wg_hi[:], wg[:], ACT.Copy).then_inc(w_hi_ready, 1)
            a.wait_ge(const_in, 16)
            a.activation(ident_b[:], cst[0:S, 0:S], ACT.Copy).then_inc(const_cast, 1)
            a.activation(mask_b[:], mask_f[0:S, :], ACT.Copy).then_inc(const_cast, 1)
            a.wait_ge(bias_in, 48)
            with a.Fori(0, NG - 1) as g:
                projections(g)
            projections(NG - 1)

            def v_high(B, s):
                a.activation(v_s[:, s, :, 0:DH], v_all[:, bass.ds(B, 1), :].rearrange("p o (h d) -> p (o h) d", d=DH),
                             ACT.Copy).then_inc(v_hi_ready, 1)

            def exps(B, j, quad):
                a.wait_ge(nm_ready, 2 * B + quad // 2 + 1)
                for h in range(4 * quad, 4 * quad + 4):
                    a.activation(prob[:, j % 2, h * S:(h + 1) * S], ps[0:S, h // 4, (h % 4) * S:(h % 4 + 1) * S], ACT.Exp,
                                 bias=nm_scaled[:, h:h + 1], scale=DH ** -0.5).then_inc(prob_ready, 1)

            def high_part(B, b):
                a.wait_ge(pt_psum, QUADS * B + b + 1)
                a.activation(pt_hi[:, b % 2, :], ps[0:S, RING[b], 0:TG], ACT.Copy).then_inc(pt_hi_ready, 1)

            def o_high(B):
                a.wait_ge(ot_psum, B + 1)
                a.activation(ot_hi[:], ps[:, 7, 8 * VX:8 * VX + KC * S].rearrange("p (k q) -> p k q", k=KC),
                             ACT.Copy).then_inc(ot_hi_ready, 1)

            def norm_out(B):
                a.wait_ge(ht_psum, B + 1)
                a.activation(h_hi_all[:, :, batch_cols(B)], ps[:, 5, 0:KC * S].rearrange("p (k q) -> p k q", k=KC),
                             ACT.Copy).then_inc(h_hi_ready, 1)
                a.activation(x1t_all[:, :, batch_cols(B)], ps[:, 5, KC * S:2 * KC * S].rearrange("p (k q) -> p k q", k=KC),
                             ACT.Copy).then_inc(x1t_ready, 1)

            def batch(B, j, turns):
                first = isinstance(B, int) and B == 0
                more = not last_batch(B)
                high_part(B, 0)
                if not first:
                    o_high(B - 1)
                high_part(B, 1)
                if not first:
                    exps(B, j, 3)
                if more:
                    exps(B + 1, j + 1, 0)
                high_part(B, 2)
                high_part(B, 3)
                if more:
                    v_high(B + 1, (j + 1) % 2)
                    exps(B + 1, j + 1, 1)
                    exps(B + 1, j + 1, 2)
                if not first:
                    norm_out(B - 1)

            a.wait_ge(v_ready, 2 * NG + 2)
            v_high(0, 0)
            for quad in range(QUADS):
                exps(0, 0, quad)
            each_batch(a, batch)
            o_high(NB - 1)
            norm_out(NB - 1)

            for c in range(NG):
                a.wait_ge(lt_psum, c + 1)
                a.activation(logit_t[:, c * TG:(c + 1) * TG], ps[0:NE, c, 0:TG], ACT.Copy).then_inc(lt_ready, 1)
            a.wait_ge(logit_psum, 1)
            a.activation(rt[:, 0, :], ps[0:S, 4, :], ACT.Tanh, scale=0.5).then_inc(tanh_ready, 1)
            def split_gu(loaded, slot):
                a.wait_ge(wr_in[slot], 16 * loaded)
                a.activation(w_hi[:, slot, 0:2 * D], w_raw[:, slot, 0:2 * D], ACT.Copy).then_inc(gu_hi, 1)

            def split_dn(loaded, slot):
                a.wait_ge(wd_in[slot], 16 * loaded)
                a.activation(w_hi[:, slot, 2 * D:], w_raw[:, slot, 2 * D:], ACT.Copy).then_inc(dn_hi, 1)

            def lead(N, s, pair):
                a.wait_ge(gu_psum, N + 1)
                a.activation(act[:, s, :], ps[:, 4 + 2 * (s % 2), 0:TG], ACT.Tanh, scale=0.5).then_inc(tanh_e, 1)

            def split(N, s, pair):
                if s % 2 == 1:
                    split_dn(pair + 1, s // 2)
                elif not (isinstance(N, int) and N // 2 + 1 >= HALVES * NX):
                    split_gu(pair + 1 + s // 2, (s // 2 + 1) % 2)

            def lag(N, s):
                a.wait_ge(weighted, N + 1)
                a.activation(a_hi[:, s, :], act[:, s, :], ACT.Copy).then_inc(a_hi_ready, 1)

            a.wait_ge(half_out, 16)
            split_gu(1, 0)
            lead(0, 0, 0)
            split(0, 0, 0)
            for i in range(2):
                a.wait_ge(cmbt_psum, i + 1)
                a.activation(comb_t[:, 2 * i * TG:2 * (i + 1) * TG].rearrange("p (c t) -> p c t", c=2),
                             ps[0:NE, 2 * i:2 * i + 2, 0:TG], ACT.Copy).then_inc(cmbt_ready, 1)
            total = HALVES * STEPS
            with a.Fori(0, total // 4 - 1) as p:
                for s in range(4):
                    k = 4 * p + s
                    lead(k + 1, (s + 1) % 4, p + (s + 1) // 4)
                    lag(k, s)
                    split(k + 1, (s + 1) % 4, p + (s + 1) // 4)
            for k in range(total - 4, total):
                if k + 1 < total:
                    lead(k + 1, (k + 1) % 4, (k + 1) // 4)
                lag(k, k % 4)
                if k + 1 < total:
                    split(k + 1, (k + 1) % 4, (k + 1) // 4)

        @block.vector
        def _(v):
            def group_stats(g):
                wait_alone(v, x_in, 16 * (g + 1), const_in, 16)
                for j in range(BG):
                    v.bn_stats(st[:, j, :], x_g[:, j, :]).then_inc(st_done, 1)
                wait_alone(v, st_done, BG * (g + 1), const_in, 16)
                for j in range(BG):
                    v.bn_aggr(mv[:, j, :], st[:, j, :]).then_inc(mv_done, 1)
                v.wait_ge(mv_done, BG * (g + 1))
                v.tensor_scalar(ve[:], mv[:, :, 1], EPS, None, ALU.add).then_inc(var_ready, 1)

            def normalise_group(g):
                v.wait_ge(rstd_ready, g + 1)
                for j in range(BG):
                    v.tensor_scalar(xn[:, j, :], x_g[:, j, :], mv[:, j, 0:1], rstd[:, j:j + 1],
                                    ALU.subtract, ALU.mult).then_inc(xn_ready, 1)

            def projections(g):
                cols = bass.ds(g * TG, TG)
                more = not (isinstance(g, int) and g == NG - 1)
                v.wait_ge(xt_hi_ready, g + 1)
                v.tensor_tensor(xt_lo[:], ps[:, 2:2 + KC, 0:TG], f(xt_hi[:]), ALU.subtract).then_inc(xt_lo_ready, 1)
                if more:
                    group_stats(g + 1)
                for m in range(KC):
                    v.wait_ge(k_hi_ready, KC * g + m + 1)
                    v.scalar_tensor_tensor(k_lo_all[:, m, cols], ps[:, m, 0:TG], cb_qk[:, 1, m:m + 1],
                                           f(k_hi_all[:, m, cols]), ALU.add, ALU.subtract).then_inc(k_lo_ready, 1)
                if more:
                    normalise_group(g + 1)
                for i in range(2):
                    v.wait_ge(v_psum, 2 * g + i + 1)
                    v.tensor_tensor(v_all[:, bass.ds(g * BG + 2 * i, 2), :],
                                    ps[0:S, 4 + i, :].rearrange("p (b d) -> p b d", b=2),
                                    rb_vo[:, 0, :].unsqueeze(1).to_broadcast([S, 2, D]), ALU.add).then_inc(v_ready, 1)
                for m in range(KC):
                    v.wait_ge(q_hi_ready, KC * g + m + 1)
                    v.scalar_tensor_tensor(q_lo_all[:, m, cols], ps[:, 6 + m, 0:TG], cb_qk[:, 0, m:m + 1],
                                           f(q_hi_all[:, m, cols]), ALU.add, ALU.subtract).then_inc(q_lo_ready, 1)

            v.sem_inc(k_lo_ready, KC)
            v.sem_inc(v_ready, 2)
            group_stats(0)
            normalise_group(0)
            for i, matrix in enumerate(WEIGHT_ORDER):
                v.wait_ge(w_hi_ready, i + 1)
                v.tensor_tensor(wa_lo[:, matrix, :, :], wa[:, matrix, :, :], f(wa_hi[:, matrix, :, :]),
                                ALU.subtract).then_inc(w_lo_ready, 1)
            v.wait_ge(w_hi_ready, 5)
            v.tensor_tensor(wg_lo[:], wg[:], f(wg_hi[:]), ALU.subtract).then_inc(w_lo_ready, 1)
            v.wait_ge(bias_in, 48)
            with v.Fori(0, NG - 1) as g:
                projections(g)
            projections(NG - 1)

            def maximum(B, i):
                v.wait_ge(score_psum, 2 * B + i + 1)
                v.tensor_reduce(nm[:, 8 * i:8 * i + 8].rearrange("p (r n) -> p r n", r=2),
                                ps[0:S, 2 * i:2 * i + 2, 0:TG].rearrange("p r (n k) -> p r n k", k=S), AX.X, ALU.max,
                                negate=True).then_inc(max_ready, 1)
                v.wait_ge(max_ready, 2 * B + i + 1)
                v.tensor_scalar(nm_scaled[:, 8 * i:8 * i + 8], nm[:, 8 * i:8 * i + 8], DH ** -0.5, None,
                                ALU.mult).then_inc(nm_ready, 1)


            def low_part(B, b):
                v.wait_ge(pt_hi_ready, QUADS * B + b + 1)
                v.tensor_tensor(pt_lo[:, b % 2, :], ps[0:S, RING[b], 0:TG], f(pt_hi[:, b % 2, :]),
                                ALU.subtract).then_inc(pt_lo_ready, 1)

            def residual(B, j):
                v.wait_ge(xr_ready, B + 1)
                v.wait_ge(proj_psum, B + 1)
                v.tensor_tensor(x1[:, j % 2, :], ps[0:S, 4, 0:D], x_r[:, j, :], ALU.add).then_inc(x1_ready, 1)

            def norm_stats(B, j):
                wait_alone(v, x1_ready, B + 1, const_in, 16)
                v.bn_stats(st2[:], x1[:, j % 2, :]).then_inc(st2_done, 1)
                wait_alone(v, st2_done, B + 1, const_in, 16)
                v.bn_aggr(mv2[:], st2[:]).then_inc(mv2_done, 1)
                v.wait_ge(mv2_done, B + 1)
                v.tensor_scalar(ve2[:], mv2[:, 1:2], EPS, None, ALU.add).then_inc(var2_ready, 1)

            def normalise(B, j):
                v.wait_ge(rstd2_ready, B + 1)
                v.tensor_scalar(h1[:, j % 2, :], x1[:, j % 2, :], mv2[:, 0:1], rstd2[:], ALU.subtract,
                                ALU.mult).then_inc(h1_ready, 1)

            def rows_out(B):
                v.wait_ge(pv_psum, B + 1)
                o = ps[0:S, 6:8, 0:8 * VX].rearrange("p b (h d) -> p b h d", d=VX)
                by_bank = lambda ap: ap.rearrange("p (b h) d -> p b h d", b=2)
                v.tensor_copy(by_bank(o_sum[:]), o[:, :, :, VW:VX]).then_inc(o_read, 1)
                v.reciprocal(rden[:].rearrange("p (b h) -> p b h", b=2), o[:, :, :, DH]).then_inc(o_read, 1)
                v.wait_ge(o_read, 4 * B + 2)
                v.tensor_tensor(by_bank(o_sum[:]), by_bank(o_sum[:]), o[:, :, :, 0:DH], ALU.add).then_inc(o_read, 2)
                v.wait_ge(o_read, 4 * B + 4)
                v.tensor_tensor(on[:].rearrange("p (h d) -> p h d", d=DH), o_sum[:],
                                rden[:].unsqueeze(2).to_broadcast([S, NH, DH]), ALU.mult).then_inc(on_ready, 1)

            def o_low(B):
                v.wait_ge(ot_hi_ready, B + 1)
                v.tensor_tensor(ot_lo[:], ps[:, 7, 8 * VX:8 * VX + KC * S].rearrange("p (k q) -> p k q", k=KC), f(ot_hi[:]),
                                ALU.subtract).then_inc(ot_lo_ready, 1)

            def norm_low(B):
                v.wait_ge(x1t_ready, B + 1)
                v.tensor_tensor(h_lo_all[:, :, batch_cols(B)], ps[:, 5, 0:KC * S].rearrange("p (k q) -> p k q", k=KC),
                                f(h_hi_all[:, :, batch_cols(B)]), ALU.subtract).then_inc(h_lo_ready, 1)

            def batch(B, j, turns):
                first = isinstance(B, int) and B == 0
                more = not last_batch(B)
                low_part(B, 0)
                if not first:
                    o_low(B - 1)
                low_part(B, 1)
                if more:
                    maximum(B + 1, 0)
                if not first:
                    residual(B - 1, (j - 1) % 4)
                    norm_stats(B - 1, (j - 1) % 4)
                low_part(B, 2)
                low_part(B, 3)
                if not first:
                    normalise(B - 1, (j - 1) % 4)
                if more:
                    maximum(B + 1, 1)
                rows_out(B)
                if not first:
                    norm_low(B - 1)

            v.sem_inc(h_lo_ready, 1)
            maximum(0, 0)
            maximum(0, 1)
            each_batch(v, batch)
            o_low(NB - 1)
            residual(NB - 1, (NB - 1) % 4)
            norm_stats(NB - 1, (NB - 1) % 4)
            normalise(NB - 1, (NB - 1) % 4)
            norm_low(NB - 1)

            done = [0]

            def then(*instructions):
                for i in instructions:
                    i.then_inc(step, 1)
                done[0] += len(instructions)
                v.wait_ge(step, done[0])

            def split_gu(count, slot):
                v.wait_ge(gu_hi, count)
                v.tensor_tensor(w_lo[:, slot, 0:2 * D], w_raw[:, slot, 0:2 * D], f(w_hi[:, slot, 0:2 * D]),
                                ALU.subtract).then_inc(gu_lo, 1)

            def route():
                R = lambda i: rt[:, i, :]
                by_group = lambda ap: ap.rearrange("p (n e) -> p n e", e=EPG)
                v.wait_ge(tanh_ready, 1)
                then(v.tensor_scalar(R(1), R(0), 0.5, 0.5, ALU.mult, ALU.add))
                then(v.tensor_tensor(R(2).rearrange("p (b e) -> p b e", e=NE), R(1).rearrange("p (b e) -> p b e", e=NE),
                                        gb[:].unsqueeze(1).to_broadcast([S, NB, NE]), ALU.add))
                pairs = R(2).rearrange("p (n t) -> p n t", t=2)
                then(v.tensor_tensor(pair_max[:].rearrange("p n t -> p (n t)"), pairs[:, :, 0], pairs[:, :, 1], ALU.max),
                     v.tensor_tensor(pair_min[:].rearrange("p n t -> p (n t)"), pairs[:, :, 0], pairs[:, :, 1], ALU.min))
                then(v.tensor_tensor(gs[:, 0, :], pair_max[:, :, 0], pair_max[:, :, 1], ALU.max),
                     v.tensor_tensor(gs[:, 1, :], pair_max[:, :, 0], pair_max[:, :, 1], ALU.min),
                     v.tensor_tensor(gs[:, 2, :], pair_min[:, :, 0], pair_min[:, :, 1], ALU.max))
                then(v.tensor_tensor(gs[:, 1, :], gs[:, 1, :], gs[:, 2, :], ALU.max))
                then(v.tensor_tensor(gs[:, 0, :], gs[:, 0, :], gs[:, 1, :], ALU.add))
                split_gu(1, 0)
                of_batch = lambda i, b: gs[:, i, b * NGRP:(b + 1) * NGRP]
                then(*[v.max(best[:, b, :], of_batch(0, b)) for b in range(NB)])
                then(v.tensor_scalar(best[:, :, TOPG:], best[:, :, TOPG:], NOWHERE, None, ALU.min))
                then(*[v.match_replace(of_batch(2, b), best[:, b, :], of_batch(0, b), TAKEN) for b in range(NB)])
                then(v.scalar_tensor_tensor(by_group(R(3)), gs[:, 2, :].unsqueeze(2).to_broadcast([S, NB * NGRP, EPG]), TAKEN,
                                            by_group(R(2)), ALU.is_equal, ALU.mult))
                part_of = lambda i, b: rt[:, i, b * NE:(b + 1) * NE]
                then(*[v.max(best[:, b, :], part_of(3, b)) for b in range(NB)])
                then(*[v.match_replace(part_of(4, b), best[:, b, :], part_of(3, b), TAKEN) for b in range(NB)])
                then(v.scalar_tensor_tensor(R(6), R(4), TAKEN, R(1), ALU.is_equal, ALU.mult))
                then(v.tensor_reduce(wsum[:, 0, :], R(6).rearrange("p (b e) -> p b e", e=NE), AX.X, ALU.add))
                then(v.tensor_scalar(wsum[:, 1, :], wsum[:, 0, :], 1e-20, None, ALU.add))
                then(v.reciprocal(wsum[:, 0, :], wsum[:, 1, :]))
                v.scalar_tensor_tensor(R(7).rearrange("p (b e) -> p b e", e=NE), R(6).rearrange("p (b e) -> p b e", e=NE),
                                       ROUTE_SCALE / 2, wsum[:, 0, :].unsqueeze(2).to_broadcast([S, NB, NE]),
                                       ALU.mult, ALU.mult).then_inc(cmb_ready, 1)

            route()

            def lead(N, s):
                v.wait_ge(tanh_e, N + 1)
                v.scalar_tensor_tensor(act[:, s, :], act[:, s, :], 1.0, ps[:, 4 + 2 * (s % 2), 0:TG], ALU.add,
                                       ALU.mult).then_inc(opened, 1)
                v.wait_ge(opened, N + 1)
                v.tensor_tensor(act[:, s, :], act[:, s, :], ps[:, 5 + 2 * (s % 2), 0:TG], ALU.mult).then_inc(gated, 1)

            def split_at(pair, s, last=False):
                if s % 2 == 1:
                    slot = s // 2
                    v.wait_ge(dn_hi, 2 * pair + slot + 1)
                    v.tensor_tensor(w_lo[:, slot, 2 * D:], w_raw[:, slot, 2 * D:], f(w_hi[:, slot, 2 * D:]),
                                    ALU.subtract).then_inc(dn_lo, 1)
                elif not last:
                    split_gu(2 * pair + s // 2 + 2, (s // 2 + 1) % 2)

            def lag(N, s):
                v.wait_ge(a_hi_ready, N + 1)
                v.tensor_tensor(a_lo[:, s, :], act[:, s, :], f(a_hi[:, s, :]), ALU.subtract).then_inc(a_lo_ready, 1)

            def outputs(h):
                for c in range(CPH):
                    v.wait_ge(down_done, STEPS * (h + 1) - CPH + c + 1)
                    for m in range(KC):
                        if h:
                            v.wait_ge(y_stored, 16 * (c * KC + m + 1))
                        v.tensor_tensor(y_out[:, c * KC + m, :], ps[:, c * KC + m, 0:TG],
                                        x1t_all[:, m, (h * CPH + c) * TG:(h * CPH + c + 1) * TG],
                                        ALU.add).then_inc(y_ready, 1)

            lead(0, 0)
            split_at(0, 0)
            total = HALVES * STEPS
            for h in range(HALVES):
                with v.Fori(h * STEPS // 4, (h + 1) * STEPS // 4 - (1 if h else 0)) as p:
                    for s in range(4):
                        k = 4 * p + s
                        lead(k + 1, (s + 1) % 4)
                        lag(k, s)
                        split_at(p + (s + 1) // 4, (s + 1) % 4)
                if h == 0:
                    outputs(0)
            for k in range(total - 4, total):
                if k + 1 < total:
                    lead(k + 1, (k + 1) % 4)
                lag(k, k % 4)
                if k + 1 < total:
                    split_at((k + 1) // 4, (k + 1) % 4, last=(k + 1) // 2 + 1 >= HALVES * NX)
            outputs(1)

        @block.tensor
        def _(t):
            def product(out, pairs):
                n = 3 * len(pairs)
                i = 0
                for w_h, w_l, m_h, m_l in pairs:
                    for w, m in ((w_h, m_h), (w_h, m_l), (w_l, m_h)):
                        last = t.matmul(out, w, m, start=(i == 0), stop=(i == n - 1))
                        i += 1
                return last

            t.wait_ge(const_in, 16)
            with t.Fori(0, NG) as g:
                t.wait_ge(xn_ready, BG * (g + 1))
                for k in range(KC):
                    for j in range(BG):
                        last = t.transpose(ps[:, 2 + k, j * S:(j + 1) * S], xn[:, j, k * P:(k + 1) * P], ident[0:S, 0:S])
                last.then_inc(xt_psum, 1)
                t.wait_ge(w_lo_ready, 1)
                t.wait_ge(k_lo_ready, KC * (g + 1))
                t.wait_ge(ctx_hi_ready, g + 1)
                t.wait_ge(ctx_lo_ready, g + 1)
                for m in range(KC):
                    w = lambda a, k: a[:, 1, k, m * P:(m + 1) * P]
                    product(ps[:, m, 0:TG], [(w(wa_hi, k), w(wa_lo, k), ctx_hi[:, k, :], ctx_lo[:, k, :])
                                             for k in range(KC)]).then_inc(k_psum, 1)
                t.wait_ge(w_lo_ready, 2)
                t.wait_ge(v_ready, 2 * (g + 1))
                for j in range(BG):
                    c = lambda a, k: a[:, k, j * S:(j + 1) * S]
                    last = product(ps[0:S, 4 + j // 2, (j % 2) * D:(j % 2 + 1) * D],
                                   [(c(ctx_hi, k), c(ctx_lo, k), wa_hi[:, 2, k, :], wa_lo[:, 2, k, :]) for k in range(KC)])
                    if j % 2:
                        last.then_inc(v_psum, 1)
                t.wait_ge(w_lo_ready, 3)
                t.wait_ge(xt_hi_ready, g + 1)
                t.wait_ge(xt_lo_ready, g + 1)
                for m in range(KC):
                    w = lambda a, k: a[:, 0, k, m * P:(m + 1) * P]
                    product(ps[:, 6 + m, 0:TG], [(w(wa_hi, k), w(wa_lo, k), xt_hi[:, k, :], xt_lo[:, k, :])
                                                 for k in range(KC)]).then_inc(q_psum, 1)

            def scores(B, j, b):
                s = j % 2
                m, n = b // 2, slice(4 * (b % 2), 4 * (b % 2) + 4)
                out = ps[0:S, b, 0:TG]
                t.matmul(out, ident_b[:], mask_b[:], start=True, stop=False, skip_group_check=True)
                for q_part, k_part in ((0, 0), (0, 1), (1, 0)):
                    last = t.matmul(out, q_now[:, s, q_part, m, :], k_blocks[:, s, k_part, m, n, :], start=False,
                                    stop=q_part == 1, skip_group_check=True)
                return last

            def half_scores(B, j, turns, i):
                if i == 0:
                    t.wait_ge(kq_in[j % 2], KQ_DMAS * 16 * (2 * turns + j // 2 + 1))
                for b in (2 * i, 2 * i + 1):
                    last = scores(B, j, b)
                last.then_inc(score_psum, 1)

            def turn(B, j, b):
                for n in range(4):
                    last = t.transpose(ps[0:S, RING[b], n * S:(n + 1) * S],
                                       prob[:, j % 2, (4 * b + n) * S:(4 * b + n + 1) * S], ident[0:S, 0:S])
                last.then_inc(pt_psum, 1)

            def values(B, j, b):
                if b == 0:
                    t.wait_ge(v_lo_ready, B + 1)
                t.wait_ge(pt_hi_ready, QUADS * B + b + 1)
                t.wait_ge(pt_lo_ready, QUADS * B + b + 1)
                for n in range(4):
                    h = 4 * b + n
                    c = slice(n * S, (n + 1) * S)
                    at = (h % 8) * VX
                    t.matmul(ps[0:S, 6 + h // 8, at:at + VX], pt_hi[:, b % 2, c], v_s[:, j % 2, h, :], start=True, stop=False,
                             skip_group_check=True)
                    last = t.matmul(ps[0:S, 6 + h // 8, at:at + VW], pt_lo[:, b % 2, c], v_s[:, j % 2, h, 0:VW], start=False,
                                    stop=True, skip_group_check=True)
                return last

            def turn_output(B):
                t.wait_ge(on_ready, B + 1)
                for k in range(KC):
                    last = t.transpose(ps[:, 7, 8 * VX + k * S:8 * VX + (k + 1) * S], on[:, k * P:(k + 1) * P], ident[0:S, 0:S])
                last.then_inc(ot_psum, 1)

            def project(B):
                t.wait_ge(ot_hi_ready, B + 1)
                t.wait_ge(ot_lo_ready, B + 1)
                product(ps[0:S, 4, 0:D], [(ot_hi[:, k, :], ot_lo[:, k, :], wa_hi[:, 3, k, :], wa_lo[:, 3, k, :])
                                          for k in range(KC)]).then_inc(proj_psum, 1)

            def turn_rows(B, j):
                t.wait_ge(h1_ready, B + 1)
                for i, rows in enumerate((h1, x1)):
                    for k in range(KC):
                        last = t.transpose(ps[:, 5, (KC * i + k) * S:(KC * i + k + 1) * S],
                                           rows[:, j % 2, k * P:(k + 1) * P], ident[0:S, 0:S])
                last.then_inc(ht_psum, 1)

            def batch(B, j, turns):
                first = isinstance(B, int) and B == 0
                more = not last_batch(B)
                ahead = (B + 1, (j + 1) % 4, turns + (j + 1) // 4)
                t.wait_ge(prob_ready, NH * B + 4)
                turn(B, j, 0)
                t.wait_ge(prob_ready, NH * B + 8)
                if more:
                    half_scores(*ahead, 0)
                if not first:
                    turn_output(B - 1)
                    t.wait_ge(h_lo_ready, B)
                turn(B, j, 1)
                values(B, j, 0)
                if not first:
                    project(B - 1)
                values(B, j, 1)
                t.wait_ge(prob_ready, NH * B + 12)
                turn(B, j, 2)
                t.wait_ge(prob_ready, NH * (B + 1))
                if not first:
                    t.wait_ge(x1_ready, B)
                turn(B, j, 3)
                if more:
                    half_scores(*ahead, 1)
                values(B, j, 2)
                values(B, j, 3).then_inc(pv_psum, 1)
                if not first:
                    turn_rows(B - 1, (j - 1) % 4)

            t.wait_ge(const_cast, 2)
            t.wait_ge(w_lo_ready, 5)
            t.wait_ge(k_lo_ready, KC * (NG + 1))
            t.wait_ge(v_pad, 3)
            half_scores(0, 0, 0, 0)
            half_scores(0, 0, 0, 1)
            each_batch(t, batch)

            def logits(c):
                t.wait_ge(h_lo_ready, BG * (c + 1) + 1)
                cols = slice(c * TG, (c + 1) * TG)
                product(ps[0:NE, c, 0:TG], [(wg_hi[:, k, :], wg_lo[:, k, :], h_hi_all[:, k, cols], h_lo_all[:, k, cols])
                                            for k in range(KC)]).then_inc(lt_psum, 1)

            logits(0)
            turn_output(NB - 1)
            logits(1)
            project(NB - 1)
            logits(2)
            t.wait_ge(h_lo_ready, NB)
            turn_rows(NB - 1, (NB - 1) % 4)
            for b in range(NB):
                if b == NB - BG:
                    logits(NG - 1)
                t.wait_ge(lt_ready, b // BG + 1)
                last = t.transpose(ps[0:S, 4, b * NE:(b + 1) * NE], logit_t[:, b * S:(b + 1) * S], ident[0:NE, 0:NE])
            last.then_inc(logit_psum, 1)
            def gate_up(N, s, col, experts):
                slot = s // 2
                if s % 2 == 0:
                    t.wait_ge(gu_hi, experts)
                    t.wait_ge(gu_lo, experts)
                if not (isinstance(N, int) and N < 2):
                    t.wait_ge(gated, N - 1)
                for part_of in range(2):
                    w = lambda a, k: a[:, slot, (2 * part_of + k) * P:(2 * part_of + k + 1) * P]
                    last = product(ps[:, 4 + 2 * (s % 2) + part_of, 0:TG],
                                   [(w(w_hi, k), w(w_lo, k), h_hi_all[:, k, col:col + TG], h_lo_all[:, k, col:col + TG])
                                    for k in range(KC)])
                last.then_inc(gu_psum, 1)

            def down(k, s, experts):
                slot = s // 2
                if s % 2 == 0:
                    t.wait_ge(dn_hi, experts)
                    t.wait_ge(dn_lo, experts)
                t.wait_ge(a_hi_ready, k + 1)
                t.wait_ge(a_lo_ready, k + 1)
                for m in range(KC):
                    w = lambda a: a[:, slot, 2 * D + m * P:2 * D + (m + 1) * P]
                    for i, (ww, mm) in enumerate(((w_hi, a_hi), (w_hi, a_lo), (w_lo, a_hi))):
                        last = t.matmul(ps[:, (s % 2) * KC + m, 0:TG], w(ww), mm[:, s, :], start=False, stop=False,
                                        skip_group_check=True)
                last.then_inc(down_done, 1)

            t.wait_ge(tanh_ready, 1)
            gate_up(0, 0, 0, 1)
            gate_up(1, 1, TG, 1)
            t.wait_ge(cmb_ready, 1)
            for b in range(NB):
                last = t.transpose(ps[0:NE, b // BG, (b % BG) * S:(b % BG + 1) * S], rt[:, 7, b * NE:(b + 1) * NE],
                                   ident[0:S, 0:S])
                if b % 8 == 7:
                    last.then_inc(cmbt_psum, 1)
            t.wait_ge(cmbt_ready, 2)
            total = HALVES * STEPS
            for h in range(HALVES):
                t.wait_ge(zero_ready, 1)
                for b in range(CPH * KC):
                    if h:
                        t.wait_ge(y_ready, b + 1)
                    t.matmul(ps[:, b, 0:TG], zero_b[:, 0:P], zero_b[:], start=True, stop=False, skip_group_check=True)
                col = lambda c, later: ((h + later) * CPH + c) * TG

                with t.Fori(h * STEPS // 4, (h + 1) * STEPS // 4 - 1) as p:
                    for s in range(4):
                        gate_up(4 * p + s + 2, (s + 2) % 4, col(s % 2, 0), 2 * p + s // 2 + 2)
                        down(4 * p + s, s, 2 * p + s // 2 + 1)
                for s in range(4):
                    N = (h + 1) * STEPS - 4 + s
                    if N + 2 < total:
                        gate_up(N + 2, (s + 2) % 4, col(s % 2, 1 if s >= 2 else 0), N // 2 + 2)
                    down(N, s, N // 2 + 1)


def constants():
    import numpy as np
    cst = np.zeros((P, CST), np.float32)
    cst[:, 0:P] = np.eye(P)
    causal = np.where(np.arange(S)[None, :] <= np.arange(S)[:, None], 0.0, MASKED)
    cst[0:S, P:P + TG] = np.tile(causal, (1, 4))
    cst[:, -BG:] = -0.5
    return cst


def kernel(x, ctx_1024, L0_xattn_Wq, L0_xattn_bq, L0_xattn_Wk, L0_xattn_bk, L0_xattn_Wv, L0_xattn_bv, L0_xattn_Wo,
           L0_xattn_bo, L0_ffn_gate_w, L0_ffn_gate_bias, L0_ffn_w_gate, L0_ffn_w_up, L0_ffn_w_down, L0_ffn_sh_gate,
           L0_ffn_sh_up, L0_ffn_sh_down):
    import numpy as np
    import concourse.bacc as bacc
    from concourse.bass_utils import run_bass_kernel_spmd

    A = np.asarray
    rows = lambda w: A(w).reshape(KC, P, -1).transpose(1, 0, 2)
    turned = lambda w: A(w).transpose(0, 2, 1)
    gate = np.concatenate([turned(A(L0_ffn_sh_gate).reshape(2, FI, D)), turned(L0_ffn_w_gate)])
    up = np.concatenate([turned(A(L0_ffn_sh_up).reshape(2, FI, D)), turned(L0_ffn_w_up)])
    down = np.concatenate([A(L0_ffn_sh_down).T.reshape(2, FI, D), turned(L0_ffn_w_down)])
    by_chunk = lambda w: w.reshape(NX, KC, P, FI).transpose(0, 2, 1, 3).reshape(NX, P, KC * FI)
    arrays = {
        "x": A(x).transpose(1, 0, 2),
        "ctx_t": A(ctx_1024)[:, :S].transpose(2, 0, 1).reshape(KC, P, T).transpose(1, 0, 2),
        "w_attn": np.stack([rows(w) for w in (L0_xattn_Wq, L0_xattn_Wk, L0_xattn_Wv, L0_xattn_Wo)], 1),
        "w_gate_t": rows(A(L0_ffn_gate_w).T),
        "col_bias": np.stack([A(b).reshape(KC, P).T for b in (L0_xattn_bq, L0_xattn_bk)], 1),
        "row_bias": np.stack([A(L0_xattn_bv), A(L0_xattn_bo)]),
        "gate_bias": A(L0_ffn_gate_bias),
        "w_exp": np.concatenate([by_chunk(gate), by_chunk(up), down], 2),
        "consts": constants(),
    }
    arrays = {k: np.ascontiguousarray(a) for k, a in arrays.items()}
    nc = bacc.Bacc("TRN2", target_bir_lowering=False, num_devices=1)
    args = [nc.dram_tensor(k, a.shape, mybir.dt.from_np(a.dtype), kind="ExternalInput").ap() for k, a in arrays.items()]
    out_t = nc.dram_tensor("out_t", (D, T), F32, kind="ExternalOutput").ap()
    block_kernel(nc, *args, out_t)
    r = run_bass_kernel_spmd(nc, [arrays], core_ids=[0])
    return np.ascontiguousarray(r.results[0]["out_t"].T).reshape(NB, S, D)
```
